# Optimizing a Trainium2 kernel written in Bass

```python
import numpy as np
import jax
import jax.numpy as jnp

def _softmax(x, axis=-1):
    return jax.nn.softmax(x, axis=axis)

def _gelu(x):
    return jax.nn.gelu(x, approximate=True)

def _silu(x):
    return jax.nn.silu(x)

def _sigmoid(x):
    return jax.nn.sigmoid(x)

def _layernorm(x, axis=-1, eps=1e-05):
    m = jnp.mean(x, axis=axis, keepdims=True)
    v = jnp.var(x, axis=axis, keepdims=True)
    return (x - m) / jnp.sqrt(v + eps)

def _scatter_add(tgt, idx, src, axis=0):
    return tgt.at[idx].add(src)

def _segment_sum(src, seg, n):
    return jax.ops.segment_sum(src, seg, n)
kernel_name = 'mk_sandwich_d1_jaxref_r2_8ec3d5'

def setup_inputs(seed: int=0):
    np.random.seed(seed)
    _w = jnp.asarray

    def _L0_attn_setup():
        import jax, jax.numpy as jnp
        import numpy as np
        import math
        INPUT_SIZE = 512
        HIDDEN = 512
        SEQ_LEN = 128
        BATCH = 128

        def _lstm(input_seq, w, u, bias):
            H = u.shape[0]
            B = input_seq.shape[1]
            x_proj = jnp.einsum('sbi,ih->sbh', input_seq, w) + bias

            def step(carry, xp_t):
                h_prev, c_prev = carry
                g = xp_t + h_prev @ u
                gates = jax.nn.sigmoid(g[:, :3 * H])
                c_cand = jnp.tanh(g[:, 3 * H:])
                ig, fg, og = (gates[:, :H], gates[:, H:2 * H], gates[:, 2 * H:])
                c = fg * c_prev + ig * c_cand
                h = og * jnp.tanh(c)
                return ((h, c), h)
            init = (jnp.zeros((B, H), dtype=input_seq.dtype), jnp.zeros((B, H), dtype=input_seq.dtype))
            _, hs = jax.lax.scan(step, init, x_proj)
            return hs
        key = jax.random.key(seed)
        k1, k2, k3, k4 = jax.random.split(key, 4)
        stddev = 1.0 / math.sqrt(HIDDEN)
        input_seq = jax.random.normal(k1, (SEQ_LEN, BATCH, INPUT_SIZE), dtype=jnp.float32)
        w = jax.random.uniform(k2, (INPUT_SIZE, 4 * HIDDEN), minval=-stddev, maxval=stddev, dtype=jnp.float32)
        u = jax.random.uniform(k3, (HIDDEN, 4 * HIDDEN), minval=-stddev, maxval=stddev, dtype=jnp.float32)
        bias = jax.random.uniform(k4, (4 * HIDDEN,), minval=-stddev, maxval=stddev, dtype=jnp.float32)
        return {'input_seq': input_seq, 'w': w, 'u': u, 'bias': bias}
    _L0_attn_in = _L0_attn_setup()

    def _L0_ffn_setup():
        import jax, jax.numpy as jnp
        import numpy as np
        B, N, D = (4, 1024, 512)
        SPARSITY = 0.01
        key = jax.random.key(seed)
        k1, k2, k3 = jax.random.split(key, 3)
        x = jax.random.normal(k1, (B, N, D), dtype=jnp.float32)
        spatial = jax.random.normal(k2, (D, D), dtype=jnp.float32) * 0.02
        freq = jnp.fft.fft(spatial, axis=-1)
        k = int(D * SPARSITY)
        mag = jnp.abs(freq)
        kth = jax.lax.top_k(mag, k)[0][:, -1:]
        w_sparse = jnp.where(mag >= kth, freq, 0.0 + 0j)
        bias = jax.random.normal(k3, (D,), dtype=jnp.float32) * 0.01
        return {'x': x, 'w_freq_real': jnp.real(w_sparse).astype(jnp.float32), 'w_freq_imag': jnp.imag(w_sparse).astype(jnp.float32), 'bias': bias}
    _L0_ffn_in = _L0_ffn_setup()
    _d = {'L0_attn_input_seq': _L0_attn_in['input_seq'], 'L0_attn_w': _L0_attn_in['w'], 'L0_attn_u': _L0_attn_in['u'], 'L0_attn_bias': _L0_attn_in['bias'], 'L0_ffn_w_freq_real': _L0_ffn_in['w_freq_real'], 'L0_ffn_w_freq_imag': _L0_ffn_in['w_freq_imag'], 'L0_ffn_bias': _L0_ffn_in['bias']}
    _x0 = _d['L0_attn_input_seq']
    _d['L0_attn_input_seq'] = jax.random.normal(jax.random.fold_in(jax.random.key(seed), 1), (8, 1024, 512), dtype=_x0.dtype)
    del _x0
    return _d

def reference(L0_attn_input_seq, L0_attn_w, L0_attn_u, L0_attn_bias, L0_ffn_w_freq_real, L0_ffn_w_freq_imag, L0_ffn_bias):

    def _L0_attn_ref(input_seq, w, u, bias):
        import jax, jax.numpy as jnp
        import numpy as np
        import math
        INPUT_SIZE = 512
        HIDDEN = 512
        SEQ_LEN = 128
        BATCH = 128

        def _lstm(input_seq, w, u, bias):
            H = u.shape[0]
            B = input_seq.shape[1]
            x_proj = jnp.einsum('sbi,ih->sbh', input_seq, w) + bias

            def step(carry, xp_t):
                h_prev, c_prev = carry
                g = xp_t + h_prev @ u
                gates = jax.nn.sigmoid(g[:, :3 * H])
                c_cand = jnp.tanh(g[:, 3 * H:])
                ig, fg, og = (gates[:, :H], gates[:, H:2 * H], gates[:, 2 * H:])
                c = fg * c_prev + ig * c_cand
                h = og * jnp.tanh(c)
                return ((h, c), h)
            init = (jnp.zeros((B, H), dtype=input_seq.dtype), jnp.zeros((B, H), dtype=input_seq.dtype))
            _, hs = jax.lax.scan(step, init, x_proj)
            return hs
        return _lstm(input_seq, w, u, bias)

    def _L0_ffn_ref(x, w_freq_real, w_freq_imag, bias):
        import jax, jax.numpy as jnp
        import numpy as np
        B, N, D = (4, 1024, 512)
        SPARSITY = 0.01
        w = jax.lax.complex(w_freq_real, w_freq_imag)
        x_freq = jnp.fft.fft(x, axis=-1)
        y_freq = jnp.einsum('bnd,do->bno', x_freq, w)
        y = jnp.real(jnp.fft.ifft(y_freq, axis=-1))
        return y + bias
    x = L0_attn_input_seq
    x = x + _layernorm(_L0_attn_ref(_layernorm(x, axis=-1), L0_attn_w, L0_attn_u, L0_attn_bias), axis=-1)
    x = x + _layernorm(_L0_ffn_ref(_layernorm(x, axis=-1), L0_ffn_w_freq_real, L0_ffn_w_freq_imag, L0_ffn_bias), axis=-1)
    return x

_drawn_inputs = setup_inputs


def setup_inputs(seed=0):
    import zlib

    import numpy as np

    out = dict(_drawn_inputs(seed))
    spreads = {}
    factors = {'L0_ffn_bias': 8.0}
    for name, (base, spread) in spreads.items():
        noise = np.random.default_rng([zlib.crc32(name.encode()), seed]).standard_normal(out[name].shape)
        drawn = base * np.exp(spread * noise) if base else spread * noise
        out[name] = jnp.asarray(drawn.astype(out[name].dtype))
    for name, factor in factors.items():
        out[name] = (out[name] * factor).astype(out[name].dtype)
    return out
```

```python
from contextlib import ExitStack

import concourse.bass as bass
from concourse import mybir

P = 128
F32 = mybir.dt.float32
F32R = mybir.dt.float32r
ALU = mybir.AluOpType
ACT = mybir.ActivationFunctionType

I, C, F, O = range(4)
COLUMN_OF_KIND = {I: 0, F: 1, O: 2, C: 3}
EPS = 1e-5


def at_least(eng, sem, value):
    if isinstance(value, int) and value <= 0:
        return
    eng.wait_ge(sem, value)


def build(nc, x, w, u, gate_bias, wf_real, wf_imag, ffn_bias, wf_real_reversed,
          wf_imag_reversed, dft, out):
    T, B, D = x.shape
    H = u.shape[0]
    KC = D // P
    NB = 512
    BLOCKS = B // NB
    Q = NB // P
    STEPS = T * BLOCKS
    TILES = STEPS * Q
    assert D == H == 512 and w.shape[1] == 4 * H and B % NB == 0 and T % 2 == 0

    x_rows = x.rearrange("t b d -> (t b) d")
    out_rows = out.rearrange("t b d -> (t b) d")
    w_rows = w.rearrange("(k p) n -> k p n", p=P)
    u_rows = u.rearrange("(k p) n -> k p n", p=P)
    x1_rows = nc.dram_tensor("x1_scratch", (T * B, D), F32, kind="Internal").ap()
    m_dram = nc.dram_tensor("m_scratch", (2, P, KC * D), F32, kind="Internal").ap()

    def row(blk, t, q):
        return t * B + (blk * NB + q * P)

    def following(blk, t):
        return (blk + 1, 0) if isinstance(t, int) and t == T - 1 else (blk, t + 1)

    def preceding(blk, t):
        return (blk - 1, T - 1) if isinstance(t, int) and t == 0 else (blk, t - 1)

    with ExitStack() as ctx:
        def sb(name, shape, dt=F32, where=ctx):
            return where.enter_context(nc.sbuf_tensor(name, shape, dt))

        def sem(name):
            return ctx.enter_context(nc.semaphore(name))

        psum = ctx.enter_context(nc.psum_tensor("psum", [P, 8, 512], F32))

        ident_r = sb("ident_r", [P, P], F32R)
        minus_half = sb("minus_half", [P, 1])
        zero_eps = sb("zero_eps", [P, 2])
        dft_scale = sb("dft_scale", [P, KC])
        bias_cols = sb("bias_cols", [P, 4 * KC])
        x_bn = sb("x_bn", [P, 6])
        x_mv = sb("x_mv", [P, 2, 2])
        x_ve = sb("x_ve", [P, 2, 1])
        x_rstd = sb("x_rstd", [P, 2, 1])
        h_bn = sb("h_bn", [P, 6])
        h_mv = sb("h_mv", [P, 2])
        h_ve = sb("h_ve", [P, 1])
        h_rstd = sb("h_rstd", [P, 1])
        x1_bn = sb("x1_bn", [P, 6])
        x1_mv = sb("x1_mv", [P, 2])
        x1_mean_ve = sb("x1_mean_ve", [P, TILES, 2])
        x1_rstd = sb("x1_rstd", [P, TILES, 1])
        x_res = sb("x_res", [P, 2, D])

        h_hi = [sb(f"h_hi{i}", [P, KC, NB], F32R) for i in range(2)]
        h_lo = [sb(f"h_lo{i}", [P, KC, NB], F32R) for i in range(2)]
        c_state = sb("c_state", [P, KC, NB])
        xn_hi = sb("xn_hi", [P, KC, NB], F32R)
        xn_lo = sb("xn_lo", [P, KC, NB], F32R)
        gate_a = sb("gate_a", [P, NB])
        gate_b = sb("gate_b", [P, NB])
        gate_c = sb("gate_c", [P, NB])
        x_tile = sb("x_tile", [P, 2, D])
        ident_made_in = gate_c[:, 0:P]
        bias_rows = gate_c[0:4 * KC, P:2 * P]
        ident = ident_r[:].bitcast(F32)
        SLOTS = 4
        CREDIT = 1
        stage = sb("stage", [P, SLOTS, 512])

        with ExitStack() as recurrence:
            w_hi = sb("w_hi", [P, KC, 4 * H], F32R, recurrence)
            w_lo = sb("w_lo", [P, KC, 4 * H], F32R, recurrence)
            with ExitStack() as making_m:
                t_hi = sb("t_hi", [P, KC, D], F32R, making_m)
                t_lo = sb("t_lo", [P, KC, D], F32R, making_m)
                wf_hi = sb("wf_hi", [P, KC, D], F32R, making_m)
                wf_lo = sb("wf_lo", [P, KC, D], F32R, making_m)
                g_hi = sb("g_hi", [P, KC, D], F32R, making_m)
                g_lo = sb("g_lo", [P, KC, D], F32R, making_m)
                raw = [[sb(f"raw{i}_{n}", [P, D], F32, making_m) for n in range(4)] for i in range(2)]
            u_hi = sb("u_hi", [P, KC, 4 * H], F32R, recurrence)
            u_lo = sb("u_lo", [P, KC, 4 * H], F32R, recurrence)
        m_hi = sb("m_hi", [P, KC, D], F32R)
        m_lo = sb("m_lo", [P, KC, D], F32R)
        ffn_bias_all = sb("ffn_bias_all", [P, D])
        RING = 8
        AHEAD = 5
        x1_tile = sb("x1_tile", [P, RING, D])
        xn2 = sb("xn2", [P, RING, D])
        xn2_hi = [sb(f"xn2_hi{i}", [P, KC, P], F32R) for i in range(2)]
        xn2_lo = [sb(f"xn2_lo{i}", [P, KC, P], F32R) for i in range(2)]
        y_tile = sb("y_tile", [P, RING, D])
        out_tile = sb("out_tile", [P, RING, D])
        y_bn = sb("y_bn", [P, 6])
        y_mv = sb("y_mv", [P, 2, 2])
        y_ve = sb("y_ve", [P, 2, 1])
        y_rstd = sb("y_rstd", [P, 2, 1])

        consts_ready = sem("consts_ready")
        stats_seen = sem("stats_seen")
        ident_zeroed = sem("ident_zeroed")
        ident_made = sem("ident_made")
        ident_r_ready = sem("ident_r_ready")
        bias_loaded = sem("bias_loaded")
        bias_turned = sem("bias_turned")
        bias_ready = sem("bias_ready")
        dft_loaded = sem("dft_loaded")
        edge_zeroed = sem("edge_zeroed")
        raw_loaded = [sem(f"raw_loaded{r}") for r in range(KC)]
        dft_hi_ready = sem("dft_hi_ready")
        dft_lo_ready = sem("dft_lo_ready")
        rows_folded = sem("rows_folded")
        cols_folded = sem("cols_folded")
        wf_hi_ready = sem("wf_hi_ready")
        wf_lo_ready = sem("wf_lo_ready")
        g_done = sem("g_done")
        g_hi_ready = sem("g_hi_ready")
        g_lo_ready = sem("g_lo_ready")
        m_done = sem("m_done")
        m_hi_ready = sem("m_hi_ready")
        m_lo_ready = sem("m_lo_ready")
        m_spilled = sem("m_spilled")
        stage_loaded = [sem(f"stage_loaded{i}") for i in range(SLOTS)]
        weight_hi_ready = sem("weight_hi_ready")
        weight_lo_ready = sem("weight_lo_ready")
        x_loaded = [sem(f"x_loaded{i}") for i in range(2)]
        x_stat = sem("x_stat")
        x_rstd_ready = sem("x_rstd_ready")
        x_normed = sem("x_normed")
        x_turned = sem("x_turned")
        xn_hi_ready = sem("xn_hi_ready")
        xn_lo_ready = sem("xn_lo_ready")
        xn_used = sem("xn_used")
        gate_done = [sem(f"gate_done_{n}") for n in "icfo"]
        gate_read = [sem(f"gate_read_{n}") for n in "icfo"]
        ic_ready = sem("ic_ready")
        fc_ready = sem("fc_ready")
        c_ready = sem("c_ready")
        tanh_c_ready = sem("tanh_c_ready")
        h_ready = sem("h_ready")
        h_hi_ready = sem("h_hi_ready")
        h_lo_ready = sem("h_lo_ready")
        h_turned = sem("h_turned")
        h_stat = sem("h_stat")
        h_rstd_ready = sem("h_rstd_ready")
        h_normed = sem("h_normed")
        x_res_loaded = [sem(f"x_res_loaded{i}") for i in range(2)]
        x1_ready = sem("x1_ready")
        x1_stat = sem("x1_stat")
        x1_rstd_ready = sem("x1_rstd_ready")
        x1_stored = [sem(f"x1_stored{i}") for i in range(2)]
        m_loaded = sem("m_loaded")
        x1_loaded = [sem(f"x1_loaded{i}") for i in range(RING)]
        xn2_ready = sem("xn2_ready")
        xn2_turned = sem("xn2_turned")
        xn2_hi_ready = sem("xn2_hi_ready")
        xn2_lo_ready = sem("xn2_lo_ready")
        y_done = sem("y_done")
        y_ready = sem("y_ready")
        y_stat = sem("y_stat")
        y_rstd_ready = sem("y_rstd_ready")
        y_normed = sem("y_normed")
        out_ready = sem("out_ready")
        out_stored = [sem(f"out_stored{i}") for i in range(RING)]

        block = ctx.enter_context(nc.Block())

        def all_steps(eng, step):
            for blk in range(BLOCKS):
                step(blk, 0, 0)
                with eng.Fori(0, T // 2 - 1) as pair:
                    step(blk, 2 * pair + 1, 1)
                    step(blk, 2 * pair + 2, 0)
                step(blk, T - 1, 1)

        def number(blk, t):
            return t + blk * T

        def gates_of(t):
            kinds = [I, C, O] if isinstance(t, int) and t == 0 else [I, C, F, O]
            return [(j, kind) for j in range(KC) for kind in kinds]

        def uses(kind, blk, t, j):
            before = KC * number(blk, t) + j
            return before - KC * (blk + (0 if isinstance(t, int) and t == 0 else 1)) if kind == F else before

        def ffn_slots(eng, slot):
            for i in range(RING):
                slot(i, i)
            with eng.Fori(1, TILES // RING - 1) as g:
                for r in range(RING):
                    slot(g * RING + r, r)
            for i in range(TILES - RING, TILES):
                slot(i, i % RING)

        def inside(i, ahead):
            return not isinstance(i, int) or i + ahead < TILES

        @block.sync
        def _(sp):
            def load_x(blk, t, q):
                tile = Q * number(blk, t) + q
                at_least(sp, x_turned, tile - 1)
                sp.dma_start(x_tile[:, q % 2, :], x_rows[bass.ds(row(blk, t, q), P), :]
                             ).then_inc(x_loaded[q % 2], 16)

            def load_residual(blk, t, q):
                sp.wait_ge(x1_stored[q % 2], 16 * (Q // 2 * number(blk, t) + q // 2 + CREDIT))
                sp.dma_start(x_res[:, q % 2, :], x_rows[bass.ds(row(blk, t, q), P), :]
                             ).then_inc(x_res_loaded[q % 2], 16)

            def store_x1(blk, t, q):
                sp.wait_ge(x1_stat, 3 * (Q * number(blk, t) + q) + 1)
                sp.dma_start(x1_rows[bass.ds(row(blk, t, q), P), :], x_res[:, q % 2, :]
                             ).then_inc(x1_stored[q % 2], 16)

            def load_weight_rows(rows, k, first):
                for n in range(4):
                    if not first:
                        sp.wait_ge(weight_lo_ready, 4 * k + n - (SLOTS - 1))
                    sp.dma_start(stage[:, n, :], rows[:, n * 512:(n + 1) * 512]).then_inc(stage_loaded[n], 16)

            def load_spectral(r):
                a, b, c, d = raw[r % 2]
                k = P * (r % 2)
                first, second = (wf_real, wf_imag) if r < 2 else (wf_imag, wf_real)
                skip = 1 if k == 0 else 0
                mirror = (wf_real_reversed, wf_imag_reversed)
                for dst, src in ((a, first), (c, second)):
                    if r == 2:
                        sp.dma_start(dst[1:P, :], src[1:P, :]).then_inc(raw_loaded[r], 16)
                    else:
                        sp.dma_start(dst[:], src[k:k + P, :]).then_inc(raw_loaded[r], 16)
                for dst, src in ((b, mirror[first is wf_imag]), (d, mirror[second is wf_imag])):
                    sp.dma_start(dst[skip:P, :], src[k + skip - 1:k + P - 1, :]).then_inc(raw_loaded[r], 16)
                if r == 2:
                    sp.dma_start(a[0:1, :], wf_real[D // 2:D // 2 + 1, :]).then_inc(raw_loaded[r], 16)
                    sp.dma_start(d[0:1, :], wf_imag[D // 2:D // 2 + 1, :]).then_inc(raw_loaded[r], 16)

            sp.dma_start(bias_rows, gate_bias.rearrange("(c p) -> c p", p=P)).then_inc(bias_loaded, 16)
            for par in range(2):
                sp.sem_inc(x1_stored[par], 16 * CREDIT)
            load_x(0, 0, 0)
            load_x(0, 0, 1)
            load_spectral(0)
            for r in range(KC):
                sp.dma_start(raw[1][r][:], dft[r * P:(r + 1) * P, :]).then_inc(dft_loaded, 16)
            load_weight_rows(w_rows[0], 0, True)
            sp.wait_ge(dft_lo_ready, KC)
            load_spectral(1)
            sp.wait_ge(cols_folded, 3 * 1)
            load_spectral(2)
            sp.wait_ge(cols_folded, 3 * 2)
            load_spectral(3)
            load_x(0, 0, 2)
            load_x(0, 0, 3)
            with sp.Fori(1, KC) as k:
                load_weight_rows(w_rows[k], k, False)
            sp.wait_ge(m_lo_ready, KC)
            sp.dma_start(m_dram[0], wf_hi[:].rearrange("p k n -> p (k n)").bitcast(F32)).then_inc(m_spilled, 16)
            sp.dma_start(m_dram[1], wf_lo[:].rearrange("p k n -> p (k n)").bitcast(F32)).then_inc(m_spilled, 16)

            def step(blk, t, par):
                s0 = isinstance(t, int) and t == 0 and blk == 0
                last = isinstance(t, int) and t == T - 1 and blk == BLOCKS - 1
                for q in range(Q):
                    if not last:
                        load_x(*following(blk, t), q)
                    if s0:
                        load_weight_rows(u_rows[q], KC + q, False)
                    else:
                        if q == 0:
                            load_residual(*preceding(blk, t), 0)
                            load_residual(*preceding(blk, t), 1)
                        else:
                            store_x1(*preceding(blk, t), q - 1)
                            if q + 1 < Q:
                                load_residual(*preceding(blk, t), q + 1)
                if not s0:
                    store_x1(*preceding(blk, t), Q - 1)

            all_steps(sp, step)

            load_residual(BLOCKS - 1, T - 1, 0)
            load_residual(BLOCKS - 1, T - 1, 1)
            sp.wait_ge(gate_done[O], KC * STEPS)
            sp.dma_start(ffn_bias_all[:], ffn_bias.partition_broadcast(P)).then_inc(m_loaded, 16)
            sp.wait_ge(m_spilled, 32)

            def load_x1(i, r):
                at_least(sp, out_ready, i - (RING - 1))
                sp.dma_start(x1_tile[:, r, :], x1_rows[bass.ds(i * P, P), :]).then_inc(x1_loaded[r], 16)

            for par in range(2):
                sp.wait_ge(x1_stored[par], 16 * ((TILES - Q) // 2 + CREDIT))
            load_x1(0, 0)
            sp.dma_start(m_hi[:].rearrange("p k n -> p (k n)").bitcast(F32), m_dram[0]).then_inc(m_loaded, 16)
            sp.dma_start(m_lo[:].rearrange("p k n -> p (k n)").bitcast(F32), m_dram[1]).then_inc(m_loaded, 16)
            for i in range(1, AHEAD):
                load_x1(i, i)

            def slot(i, r):
                if inside(i, AHEAD):
                    load_x1(i + AHEAD, (r + AHEAD) % RING)
                if isinstance(i, int) and i < Q:
                    store_x1(BLOCKS - 1, T - 1, i)
                    if i + 2 < Q:
                        load_residual(BLOCKS - 1, T - 1, i + 2)
                    if i == Q - 1:
                        for par in range(2):
                            sp.wait_ge(x1_stored[par], 16 * (TILES // 2 + CREDIT))

            ffn_slots(sp, slot)

        @block.tensor
        def _(pe):
            def product(bank, lhs_hi, lhs_lo, rhs_hi, rhs_lo, start, stop):
                pe.matmul(bank, lhs_hi, rhs_hi, start=start, stop=False)
                pe.matmul(bank, lhs_hi, rhs_lo, start=False, stop=False)
                return pe.matmul(bank, lhs_lo, rhs_hi, start=False, stop=stop)

            def turn_x(blk, t, q):
                tile = Q * number(blk, t) + q
                pe.wait_ge(x_normed, tile + 1)
                for k in range(KC):
                    mm = pe.transpose(psum[:, 4 + q, k * P:(k + 1) * P], x_tile[:, q % 2, k * P:(k + 1) * P],
                                      ident)
                mm.then_inc(x_turned, 1)

            def turn_h(blk, t, q, par, bank):
                pe.wait_ge(h_lo_ready, KC * number(blk, t) + KC)
                for k in range(KC):
                    for part in (h_hi, h_lo):
                        mm = pe.matmul(psum[:, bank, k * P:(k + 1) * P], part[par][:, k, q * P:(q + 1) * P],
                                       ident_r[:], start=(part is h_hi), stop=(part is h_lo))
                mm.then_inc(h_turned, 1)

            pe.wait_ge(ident_r_ready, 1)
            pe.wait_ge(bias_loaded, 16)
            pe.transpose(psum[:, 0, 0:4 * KC], bias_rows, ident_r[0:4 * KC, 0:4 * KC].bitcast(F32)
                         ).then_inc(bias_turned, 1)
            turn_x(0, 0, 0)
            turn_x(0, 0, 1)
            pe.wait_ge(dft_lo_ready, KC)
            pe.wait_ge(bias_ready, 1)
            for r in range(KC):
                pe.wait_ge(wf_lo_ready, r + 1)
                for jj in range(KC):
                    mm = product(psum[:, jj, :], wf_hi[:, r, jj * P:(jj + 1) * P], wf_lo[:, r, jj * P:(jj + 1) * P],
                                 t_hi[:, r, :], t_lo[:, r, :], r == 0, r == KC - 1)
                    if r == KC - 1:
                        mm.then_inc(g_done, 1)
            turn_x(0, 0, 2)
            turn_x(0, 0, 3)
            pe.wait_ge(g_lo_ready, KC)
            for dc in range(KC):
                for jj in range(KC):
                    mm = product(psum[:, dc, :], g_hi[:, jj, dc * P:(dc + 1) * P], g_lo[:, jj, dc * P:(dc + 1) * P],
                                 t_hi[:, jj, :], t_lo[:, jj, :], jj == 0, jj == KC - 1)
                mm.then_inc(m_done, 1)

            def step(blk, t, par):
                s = number(blk, t)
                first = isinstance(t, int) and t == 0
                last = isinstance(t, int) and t == T - 1 and blk == BLOCKS - 1
                gates = gates_of(t)

                def x_part(j, kind):
                    pe.wait_ge(gate_read[kind], uses(kind, blk, t, j) + CREDIT)
                    col = COLUMN_OF_KIND[kind] * H + j * P
                    for k in range(KC):
                        mm = product(psum[:, kind, :], w_hi[:, k, col:col + P], w_lo[:, k, col:col + P],
                                     xn_hi[:, k, :], xn_lo[:, k, :], k == 0, first and k == KC - 1)
                    return mm

                def h_part(j, kind, fresh=False):
                    col = COLUMN_OF_KIND[kind] * H + j * P
                    for k in range(KC):
                        if fresh:
                            pe.wait_ge(h_lo_ready, KC * (s - 1) + k + 1)
                        mm = product(psum[:, kind, :], u_hi[:, k, col:col + P], u_lo[:, k, col:col + P],
                                     h_hi[1 - par][:, k, :], h_lo[1 - par][:, k, :], False, k == KC - 1)
                    mm.then_inc(gate_done[kind], 1)

                turn_h_after = {n: q for q, n in enumerate((1, 3, 6, 8) if first else (1, 4, 7, 10))}
                turn_x_after = {n: q for q, n in enumerate((2, 4, 7, 9) if first else (3, 6, 9, 12))}
                pe.wait_ge(xn_lo_ready, Q * s + Q)
                if first and blk == 0:
                    pe.wait_ge(m_lo_ready, KC)
                    pe.wait_ge(weight_lo_ready, 4 * KC)
                if not first and blk == 0 and par == 1:
                    pe.wait_ge(weight_lo_ready, 8 * KC)
                for n, (j, kind) in enumerate(gates[:-2]):
                    mm = x_part(j, kind)
                    if first:
                        mm.then_inc(gate_done[kind], 1)
                    else:
                        h_part(j, kind, fresh=(n == 0))
                    if n in turn_h_after and not (first and blk == 0):
                        q = turn_h_after[n]
                        tile = Q * number(*preceding(blk, t)) + q
                        pe.wait_ge(x1_ready, tile + CREDIT)
                        turn_h(*preceding(blk, t), q, 1 - par, 7)
                    if n in turn_x_after and not last:
                        q = turn_x_after[n]
                        if q == Q - 1 and not (first and blk == 0):
                            pe.wait_ge(x1_ready, Q * s + CREDIT)
                        turn_x(*following(blk, t), q)
                pending = gates[-2:]
                for j, kind in pending:
                    mm = x_part(j, kind)
                    if first:
                        mm.then_inc(gate_done[kind], 1)
                if not first:
                    mm.then_inc(xn_used, 1)
                    for j, kind in pending:
                        h_part(j, kind)

            all_steps(pe, step)

            for q in range(Q):
                turn_h(BLOCKS - 1, T - 1, q, 1, 4 + q)

            def turn_xn2(i, r):
                pe.wait_ge(xn2_ready, i + 1)
                at_least(pe, xn2_lo_ready, i - 1)
                for k in range(KC):
                    mm = pe.transpose(psum[:, 2 + r % 2, k * P:(k + 1) * P], xn2[:, r, k * P:(k + 1) * P], ident)
                mm.then_inc(xn2_turned, 1)

            for kind in (I, C, F, O):
                pe.wait_ge(gate_read[kind], uses(kind, BLOCKS - 1, T - 1, KC - 1) + 1 + CREDIT)
            turn_xn2(0, 0)
            pe.wait_ge(m_loaded, 48)

            def slot(i, r):
                if inside(i, 1):
                    turn_xn2(i + 1, (r + 1) % RING)
                pe.wait_ge(xn2_lo_ready, i + 1)
                at_least(pe, y_ready, i - 1)
                hi, lo = xn2_hi[r % 2], xn2_lo[r % 2]
                for k in range(KC):
                    mm = product(psum[:, r % 2, :], hi[:, k, :], lo[:, k, :], m_hi[:, k, :], m_lo[:, k, :],
                                 k == 0, k == KC - 1)
                mm.then_inc(y_done, 1)

            ffn_slots(pe, slot)

        @block.scalar
        def _(act):
            for kind in (I, C, F, O):
                act.sem_inc(gate_read[kind], CREDIT)
            act.wait_ge(bias_turned, 1)
            act.copy(bias_cols[:], psum[:, 0, 0:4 * KC]).then_inc(bias_ready, 1)
            for r in range(KC):
                act.wait_ge(dft_loaded, 16 * KC)
                act.copy(t_hi[:, r, :], raw[1][r][:]).then_inc(dft_hi_ready, 1)

            def folded_hi(r):
                act.wait_ge(cols_folded, 3 * (r + 1))
                act.copy(wf_hi[:, r, :], (gate_a, gate_b)[r % 2][:]).then_inc(wf_hi_ready, 1)

            def weight_hi(dst, k, index):
                for n in range(4):
                    act.wait_ge(stage_loaded[n], 16 * (index + 1))
                    act.copy(dst[:, k, n * 512:(n + 1) * 512], stage[:, n, :]).then_inc(weight_hi_ready, 1)

            folded_hi(0)
            weight_hi(w_hi, 0, 0)
            folded_hi(1)
            folded_hi(2)
            folded_hi(3)
            weight_hi(w_hi, 1, 1)
            act.wait_ge(consts_ready, 6)
            for jj in range(KC):
                act.wait_ge(g_done, jj + 1)
                act.activation(g_hi[:, jj, :], psum[:, jj, :], ACT.Copy, scale=dft_scale[:, jj:jj + 1]
                               ).then_inc(g_hi_ready, 1)
            with act.Fori(2, KC) as k:
                weight_hi(w_hi, k, k)
            for dc in range(KC):
                act.wait_ge(m_done, dc + 1)
                act.copy(wf_hi[:, dc, :], psum[:, dc, :]).then_inc(m_hi_ready, 1)

            def input_hi(blk, t, q):
                act.wait_ge(x_turned, Q * number(blk, t) + q + 1)
                act.copy(xn_hi[:, :, q * P:(q + 1) * P], psum[:, 4 + q, :].rearrange("p (k n) -> p k n", k=KC)
                         ).then_inc(xn_hi_ready, 1)

            for q in range(Q):
                input_hi(0, 0, q)

            def step(blk, t, par):
                s = number(blk, t)
                first = isinstance(t, int) and t == 0
                last = isinstance(t, int) and t == T - 1 and blk == BLOCKS - 1

                def gate(j, kind, dst):
                    act.wait_ge(gate_done[kind], uses(kind, blk, t, j) + 1)
                    col = COLUMN_OF_KIND[kind] * KC + j
                    act.activation(dst[:], psum[:, kind, :], ACT.Tanh if kind == C else ACT.Sigmoid,
                                   bias=bias_cols[:, col:col + 1]).then_inc(gate_read[kind], 1)

                for j in range(KC):
                    n = KC * s + j
                    at_least(act, h_lo_ready, n)
                    gate(j, I, gate_a)
                    gate(j, C, gate_b)
                    if j == KC - 1 and not last:
                        if first:
                            act.wait_ge(gate_done[O], uses(O, blk, t, j) + 1)
                        else:
                            act.wait_ge(xn_used, s - blk)
                        for q in range(Q):
                            input_hi(*following(blk, t), q)
                    if not first:
                        gate(j, F, gate_c)
                    act.wait_ge(c_ready, n + 1)
                    act.activation(gate_b[:], c_state[:, j, :], ACT.Tanh).then_inc(tanh_c_ready, 1)
                    gate(j, O, gate_c)
                    act.wait_ge(h_ready, n + 1)
                    act.copy(h_hi[par][:, j, :], gate_a[:]).then_inc(h_hi_ready, 1)
                    if first and blk == 0:
                        if j == 0:
                            act.wait_ge(m_spilled, 32)
                        weight_hi(u_hi, j, KC + j)

            all_steps(act, step)

            def store_out(i, r):
                act.wait_ge(out_ready, i + 1)
                act.dma_start(out_rows[bass.ds(i * P, P), :], out_tile[:, r, :]).then_inc(out_stored[r], 16)

            def slot(i, r):
                if inside(i, 1):
                    xn2_part(i + 1, r + 1)
                if not (isinstance(i, int) and i < 2):
                    store_out(i - 2, (r - 2) % RING)

            def xn2_part(i, r):
                act.wait_ge(xn2_turned, i + 1)
                at_least(act, y_done, i - 1)
                act.copy(xn2_hi[r % 2][:].rearrange("p k n -> p (k n)"), psum[:, 2 + r % 2, :]
                         ).then_inc(xn2_hi_ready, 1)

            xn2_part(0, 0)
            ffn_slots(act, slot)
            for i in (TILES - 2, TILES - 1):
                store_out(i, i % RING)
            for r in range(RING):
                act.wait_ge(out_stored[r], 16 * TILES // RING)

        @block.vector
        def _(dve):
            dve.sem_inc(x1_ready, CREDIT)
            dve.wait_ge(ident_made, 1)
            dve.tensor_copy(ident_r[:], ident_made_in).then_inc(ident_r_ready, 1)
            dve.wait_ge(consts_ready, 6)

            def norm_x(blk, t, q):
                tile = Q * number(blk, t) + q
                b = q % 2
                dve.wait_ge(x_loaded[b], 16 * (Q // 2 * number(blk, t) + q // 2 + 1))
                dve.bn_stats(x_bn[:], x_tile[:, b, :]).then_inc(x_stat, 1)
                dve.wait_ge(x_stat, 3 * tile + 1)
                dve.sem_inc(stats_seen, 1)
                dve.bn_aggr(x_mv[:, b, :], x_bn[:]).then_inc(x_stat, 1)
                dve.wait_ge(x_stat, 3 * tile + 2)
                dve.tensor_scalar_add(x_ve[:, b, :], x_mv[:, b, 1:2], EPS).then_inc(x_stat, 1)
                dve.wait_ge(x_rstd_ready, tile + 1)
                dve.tensor_scalar(x_tile[:, b, :], x_tile[:, b, :], x_mv[:, b, 0:1], x_rstd[:, b, :],
                                  ALU.subtract, ALU.mult).then_inc(x_normed, 1)

            def input_lo(blk, t, q):
                dve.wait_ge(xn_hi_ready, Q * number(blk, t) + q + 1)
                part = (slice(None), slice(None), slice(q * P, (q + 1) * P))
                dve.tensor_sub(xn_lo[part], psum[:, 4 + q, :].rearrange("p (k n) -> p k n", k=KC),
                               xn_hi[part].bitcast(F32)).then_inc(xn_lo_ready, 1)

            def fold(r):
                a, b, c, d = raw[r % 2]
                op = ALU.add if r < 2 else ALU.subtract
                dve.wait_ge(raw_loaded[r], 16 * (6 if r == 2 else 4))
                dve.wait_ge(edge_zeroed, 3 if r == 2 else 2)
                dve.tensor_tensor(a[:], a[:], b[:], op).then_inc(rows_folded, 1)
                dve.tensor_tensor(c[:], d[:], c[:], op).then_inc(rows_folded, 1)
                dve.wait_ge(rows_folded, 2 * r + 2)
                at_least(dve, wf_lo_ready, r - 1)
                f = (gate_a, gate_b)[r % 2]
                half = D // 2
                dve.tensor_copy(f[:, 0:D:half], a[:, 0:D:half]).then_inc(cols_folded, 1)
                dve.tensor_tensor(f[:, 1:half], a[:, 1:half], a[:, D - 1:half:-1], ALU.add).then_inc(cols_folded, 1)
                dve.tensor_tensor(f[:, half + 1:D], c[:, 1:half], c[:, D - 1:half:-1], ALU.subtract
                                  ).then_inc(cols_folded, 1)

            def folded_lo(r):
                dve.wait_ge(wf_hi_ready, r + 1)
                dve.tensor_sub(wf_lo[:, r, :], (gate_a, gate_b)[r % 2][:], wf_hi[:, r, :].bitcast(F32)
                               ).then_inc(wf_lo_ready, 1)

            def weight_lo(dst_hi, dst, k, index):
                for n in range(4):
                    dve.wait_ge(weight_hi_ready, 4 * index + n + 1)
                    cols = slice(n * 512, (n + 1) * 512)
                    dve.tensor_sub(dst[:, k, cols], stage[:, n, :], dst_hi[:, k, cols].bitcast(F32)
                                   ).then_inc(weight_lo_ready, 1)

            norm_x(0, 0, 0)
            norm_x(0, 0, 1)
            for r in range(KC):
                dve.wait_ge(dft_hi_ready, r + 1)
                dve.tensor_sub(t_lo[:, r, :], raw[1][r][:], t_hi[:, r, :].bitcast(F32)).then_inc(dft_lo_ready, 1)
            fold(0)
            folded_lo(0)
            weight_lo(w_hi, w_lo, 0, 0)
            for r in range(1, KC):
                fold(r)
                folded_lo(r)
            norm_x(0, 0, 2)
            norm_x(0, 0, 3)
            weight_lo(w_hi, w_lo, 1, 1)
            for jj in range(KC):
                dve.wait_ge(g_hi_ready, jj + 1)
                dve.scalar_tensor_tensor(out=g_lo[:, jj, :], in0=psum[:, jj, :], scalar=dft_scale[:, jj:jj + 1],
                                         in1=g_hi[:, jj, :].bitcast(F32), op0=ALU.mult, op1=ALU.subtract
                                         ).then_inc(g_lo_ready, 1)
            with dve.Fori(2, KC) as k:
                weight_lo(w_hi, w_lo, k, k)
            for dc in range(KC):
                dve.wait_ge(m_hi_ready, dc + 1)
                dve.tensor_sub(wf_lo[:, dc, :], psum[:, dc, :], wf_hi[:, dc, :].bitcast(F32)).then_inc(m_lo_ready, 1)
            for q in range(Q):
                input_lo(0, 0, q)

            def residual(blk, t, q, bank):
                tile = Q * number(blk, t) + q
                b = q % 2
                dve.wait_ge(h_turned, tile + 1)
                dve.bn_stats(h_bn[:], psum[:, bank, :]).then_inc(h_stat, 1)
                dve.wait_ge(h_stat, 3 * tile + 1)
                dve.sem_inc(stats_seen, 1)
                dve.bn_aggr(h_mv[:], h_bn[:]).then_inc(h_stat, 1)
                dve.wait_ge(h_stat, 3 * tile + 2)
                dve.tensor_scalar_add(h_ve[:], h_mv[:, 1:2], EPS).then_inc(h_stat, 1)
                dve.wait_ge(h_rstd_ready, tile + 1)
                dve.tensor_scalar(psum[:, bank, :], psum[:, bank, :], h_mv[:, 0:1], h_rstd[:],
                                  ALU.subtract, ALU.mult).then_inc(h_normed, 1)
                dve.wait_ge(h_normed, tile + 1)
                dve.wait_ge(x_res_loaded[b], 16 * (Q // 2 * number(blk, t) + q // 2 + 1))
                dve.tensor_tensor(x_res[:, b, :], psum[:, bank, :], x_res[:, b, :], ALU.add).then_inc(x1_ready, 1)
                dve.wait_ge(x1_ready, tile + 1 + CREDIT)
                dve.bn_stats(x1_bn[:], x_res[:, b, :]).then_inc(x1_stat, 1)
                dve.wait_ge(x1_stat, 3 * tile + 1)
                dve.sem_inc(stats_seen, 1)
                dve.bn_aggr(x1_mv[:], x1_bn[:]).then_inc(x1_stat, 1)
                dve.wait_ge(x1_stat, 3 * tile + 2)
                at = t * (B // P) + (blk * Q + q)
                dve.tensor_tensor(x1_mean_ve[:, bass.ds(at, 1), :].rearrange("p a b -> p (a b)"), x1_mv[:],
                                  zero_eps[:], ALU.add).then_inc(x1_stat, 1)

            def step(blk, t, par):
                s = number(blk, t)
                first = isinstance(t, int) and t == 0
                start = first and blk == 0
                last = isinstance(t, int) and t == T - 1 and blk == BLOCKS - 1
                for j in range(KC):
                    n = KC * s + j
                    if not last:
                        norm_x(*following(blk, t), j)
                    dve.wait_ge(gate_read[I], n + 1 + CREDIT)
                    dve.wait_ge(gate_read[C], n + 1 + CREDIT)
                    if first:
                        dve.tensor_mul(c_state[:, j, :], gate_a[:], gate_b[:]).then_inc(c_ready, 1)
                    else:
                        dve.tensor_mul(gate_a[:], gate_a[:], gate_b[:]).then_inc(ic_ready, 1)
                    if not start and j < 3:
                        residual(*preceding(blk, t), j, 7)
                    if j == KC - 1 and not last:
                        for q in range(Q):
                            input_lo(*following(blk, t), q)
                    if not first:
                        done = uses(F, blk, t, j) + 1
                        dve.wait_ge(gate_read[F], done + CREDIT)
                        dve.tensor_mul(gate_c[:], gate_c[:], c_state[:, j, :]).then_inc(fc_ready, 1)
                        dve.wait_ge(fc_ready, done)
                        dve.wait_ge(ic_ready, done)
                        dve.tensor_add(c_state[:, j, :], gate_c[:], gate_a[:]).then_inc(c_ready, 1)
                    dve.wait_ge(tanh_c_ready, n + 1)
                    dve.wait_ge(gate_read[O], n + 1 + CREDIT)
                    dve.tensor_mul(gate_a[:], gate_b[:], gate_c[:]).then_inc(h_ready, 1)
                    dve.wait_ge(h_hi_ready, n + 1)
                    dve.tensor_sub(h_lo[par][:, j, :], gate_a[:], h_hi[par][:, j, :].bitcast(F32)
                                   ).then_inc(h_lo_ready, 1)
                    if not start and j == 2:
                        residual(*preceding(blk, t), 3, 7)
                    if start:
                        weight_lo(u_hi, u_lo, j, KC + j)

            all_steps(dve, step)

            dve.wait_ge(m_loaded, 16)

            def norm_x1(i, r):
                dve.wait_ge(x1_loaded[r], 2 * (i - r) + 16)
                at_least(dve, xn2_turned, i - (RING - 1))
                if isinstance(i, int) and i == 0:
                    dve.wait_ge(x1_rstd_ready, TILES - Q)
                dve.tensor_scalar(xn2[:, r, :], x1_tile[:, r, :],
                                  x1_mean_ve[:, bass.ds(i, 1), 0:1].rearrange("p a b -> p (a b)"),
                                  x1_rstd[:, bass.ds(i, 1), :].rearrange("p a b -> p (a b)"),
                                  ALU.subtract, ALU.mult).then_inc(xn2_ready, 1)

            def lo_xn2(i, r):
                dve.wait_ge(xn2_hi_ready, i + 1)
                dve.tensor_sub(xn2_lo[r % 2][:].rearrange("p k n -> p (k n)"), psum[:, 2 + r % 2, :],
                               xn2_hi[r % 2][:].rearrange("p k n -> p (k n)").bitcast(F32)).then_inc(xn2_lo_ready, 1)

            def y_norm(i, r):
                dve.wait_ge(y_rstd_ready, i + 1)
                at_least(dve, out_ready, i - (RING - 1))
                dve.tensor_scalar(y_tile[:, r, :], y_tile[:, r, :], y_mv[:, r % 2, 0:1], y_rstd[:, r % 2, :],
                                  ALU.subtract, ALU.mult).then_inc(y_normed, 1)

            norm_x1(0, 0)
            norm_x1(1, 1)
            lo_xn2(0, 0)

            def slot(i, r):
                if inside(i, 2):
                    norm_x1(i + 2, (r + 2) % RING)
                if inside(i, 1):
                    lo_xn2(i + 1, (r + 1) % RING)
                if isinstance(i, int) and i < Q:
                    residual(BLOCKS - 1, T - 1, i, 4 + i)
                b = r % 2
                dve.wait_ge(y_done, i + 1)
                at_least(dve, out_ready, i - (RING - 1))
                dve.tensor_add(y_tile[:, r, :], psum[:, b, :], ffn_bias_all[:]).then_inc(y_ready, 1)
                dve.wait_ge(y_ready, i + 1)
                dve.bn_stats(y_bn[:], y_tile[:, r, :]).then_inc(y_stat, 1)
                at_least(dve, y_normed, i - 1)
                dve.wait_ge(y_stat, 3 * i + 1)
                dve.sem_inc(stats_seen, 1)
                dve.bn_aggr(y_mv[:, b, :], y_bn[:]).then_inc(y_stat, 1)
                dve.wait_ge(y_stat, 3 * i + 2)
                dve.tensor_scalar_add(y_ve[:, b, :], y_mv[:, b, 1:2], EPS).then_inc(y_stat, 1)
                if not (isinstance(i, int) and i == 0):
                    y_norm(i - 1, (r - 1) % RING)
                if isinstance(i, int) and i == Q - 1:
                    dve.wait_ge(x1_rstd_ready, TILES)

            ffn_slots(dve, slot)
            y_norm(TILES - 1, (TILES - 1) % RING)

        @block.gpsimd
        def _(pool):
            pool.memset(ident_made_in, 0.0).then_inc(ident_zeroed, 1)
            pool.wait_ge(ident_zeroed, 1)
            pool.affine_select(out=ident_made_in, in_=ident_made_in, compare_op=ALU.not_equal, fill=1.0, base=0,
                               pattern=[[-1, P]], channel_multiplier=1).then_inc(ident_made, 1)
            pool.memset(minus_half[:], -0.5).then_inc(consts_ready, 1)
            pool.wait_ge(consts_ready, 1)
            pool.memset(zero_eps[:, 0:1], 0.0).then_inc(consts_ready, 1)
            pool.memset(zero_eps[:, 1:2], EPS).then_inc(consts_ready, 1)
            pool.memset(dft_scale[:, 0:KC // 2], 1.0 / D).then_inc(consts_ready, 1)
            pool.memset(dft_scale[:, KC // 2:KC], -1.0 / D).then_inc(consts_ready, 1)
            pool.wait_ge(consts_ready, 5)
            pool.memset(dft_scale[0:1, KC // 2:KC // 2 + 1], 1.0 / D).then_inc(consts_ready, 1)
            pool.memset(raw[0][1][0:1, :], 0.0).then_inc(edge_zeroed, 1)
            pool.memset(raw[0][3][0:1, :], 0.0).then_inc(edge_zeroed, 1)

            def rstd_x(blk, t, q):
                tile = Q * number(blk, t) + q
                pool.wait_ge(x_stat, 3 * tile + 3)
                pool.tensor_tensor(x_rstd[:, q % 2, :], x_ve[:, q % 2, :], minus_half[:], ALU.pow
                                   ).then_inc(x_rstd_ready, 1)

            def rstd_residual(blk, t, q):
                tile = Q * number(blk, t) + q
                pool.wait_ge(h_stat, 3 * tile + 3)
                pool.tensor_tensor(h_rstd[:], h_ve[:], minus_half[:], ALU.pow).then_inc(h_rstd_ready, 1)
                pool.wait_ge(x1_stat, 3 * tile + 3)
                at = t * (B // P) + (blk * Q + q)
                pool.tensor_tensor(x1_rstd[:, bass.ds(at, 1), :].rearrange("p a b -> p (a b)"),
                                   x1_mean_ve[:, bass.ds(at, 1), 1:2].rearrange("p a b -> p (a b)"),
                                   minus_half[:], ALU.pow).then_inc(x1_rstd_ready, 1)

            rstd_x(0, 0, 0)
            rstd_x(0, 0, 1)
            pool.wait_ge(cols_folded, 3)
            pool.memset(raw[0][2][0:1, :], 0.0).then_inc(edge_zeroed, 1)
            rstd_x(0, 0, 2)
            rstd_x(0, 0, 3)

            def step(blk, t, par):
                start = isinstance(t, int) and t == 0 and blk == 0
                last = isinstance(t, int) and t == T - 1 and blk == BLOCKS - 1
                for j in range(KC):
                    if not last:
                        rstd_x(*following(blk, t), j)
                    if not start and j < 3:
                        rstd_residual(*preceding(blk, t), j)
                    if not start and j == 2:
                        rstd_residual(*preceding(blk, t), 3)

            all_steps(pool, step)

            def add_up(i, r):
                pool.wait_ge(y_normed, i + 1)
                at_least(pool, out_stored[r], 2 * (i - r))
                pool.tensor_tensor(out_tile[:, r, :], y_tile[:, r, :], x1_tile[:, r, :], ALU.add
                                   ).then_inc(out_ready, 1)

            def slot(i, r):
                if isinstance(i, int) and i < Q:
                    rstd_residual(BLOCKS - 1, T - 1, i)
                pool.wait_ge(y_stat, 3 * i + 3)
                pool.tensor_tensor(y_rstd[:, r % 2, :], y_ve[:, r % 2, :], minus_half[:], ALU.pow
                                   ).then_inc(y_rstd_ready, 1)
                if not (isinstance(i, int) and i == 0):
                    add_up(i - 1, (r - 1) % RING)

            ffn_slots(pool, slot)
            add_up(TILES - 1, (TILES - 1) % RING)


_INS = ["L0_attn_input_seq", "L0_attn_w", "L0_attn_u", "L0_attn_bias",
        "L0_ffn_w_freq_real", "L0_ffn_w_freq_imag", "L0_ffn_bias"]


def _real_fourier_basis(n):
    import numpy as np

    kd = np.outer(np.arange(n // 2 + 1), np.arange(n)) % n
    angle = 2.0 * np.pi * kd / n
    return np.concatenate([np.cos(angle), np.sin(angle[1:n // 2])]).astype(np.float32)


def kernel(**inputs):
    import numpy as _np
    import concourse.bacc as _bacc
    from concourse import mybir as _mybir
    from concourse.bass_utils import run_bass_kernel_spmd as _run

    nc = _bacc.Bacc("TRN2", target_bir_lowering=False, num_devices=1)
    arrays, args = {}, []
    for name in _INS:
        a = _np.ascontiguousarray(inputs[name])
        arrays[f"in_{name}_dram"] = a
        args.append(nc.dram_tensor(f"in_{name}_dram", a.shape, _mybir.dt.from_np(a.dtype), kind="ExternalInput").ap())
    for name in ("L0_ffn_w_freq_real", "L0_ffn_w_freq_imag"):
        a = _np.ascontiguousarray(inputs[name][::-1])
        arrays[f"in_{name}_reversed_dram"] = a
        args.append(nc.dram_tensor(f"in_{name}_reversed_dram", a.shape, _mybir.dt.from_np(a.dtype),
                                   kind="ExternalInput").ap())
    basis = _real_fourier_basis(inputs["L0_ffn_w_freq_real"].shape[0])
    arrays["fourier_basis_dram"] = basis
    args.append(nc.dram_tensor("fourier_basis_dram", basis.shape, _mybir.dt.float32, kind="ExternalInput").ap())
    shape = tuple(inputs["L0_attn_input_seq"].shape)
    args.append(nc.dram_tensor("out_0_dram", shape, _mybir.dt.float32, kind="ExternalOutput").ap())
    build(nc, *args)
    r = _run(nc, [arrays], core_ids=[0])
    return r.results[0]["out_0_dram"]
```

```python
from contextlib import ExitStack

import concourse.bass as bass
from concourse import mybir

P = 128
F32 = mybir.dt.float32
F32R = mybir.dt.float32r
ALU = mybir.AluOpType
ACT = mybir.ActivationFunctionType

I, C, F, O = range(4)
COLUMN_OF_KIND = {I: 0, F: 1, O: 2, C: 3}
EPS = 1e-5


def at_least(eng, sem, value):
    if isinstance(value, int) and value <= 0:
        return
    eng.wait_ge(sem, value)


def build(nc, x, w, u, gate_bias, wf_real, wf_imag, ffn_bias, wf_real_reversed,
          wf_imag_reversed, dft, out):
    T, B, D = x.shape
    H = u.shape[0]
    KC = D // P
    NB = 512
    BLOCKS = B // NB
    Q = NB // P
    STEPS = T * BLOCKS
    TILES = STEPS * Q
    assert D == H == 512 and w.shape[1] == 4 * H and B % NB == 0 and T % 2 == 0

    x_rows = x.rearrange("t b d -> (t b) d")
    out_rows = out.rearrange("t b d -> (t b) d")
    w_rows = w.rearrange("(k p) n -> k p n", p=P)
    u_rows = u.rearrange("(k p) n -> k p n", p=P)
    x1_rows = nc.dram_tensor("x1_scratch", (T * B, D), F32, kind="Internal").ap()
    m_dram = nc.dram_tensor("m_scratch", (2, P, KC * D), F32, kind="Internal").ap()

    def row(blk, t, q):
        return t * B + (blk * NB + q * P)

    def following(blk, t):
        return (blk + 1, 0) if isinstance(t, int) and t == T - 1 else (blk, t + 1)

    def preceding(blk, t):
        return (blk - 1, T - 1) if isinstance(t, int) and t == 0 else (blk, t - 1)

    with ExitStack() as ctx:
        def sb(name, shape, dt=F32, where=ctx):
            return where.enter_context(nc.sbuf_tensor(name, shape, dt))

        def sem(name):
            return ctx.enter_context(nc.semaphore(name))

        psum = ctx.enter_context(nc.psum_tensor("psum", [P, 8, 512], F32))

        ident_r = sb("ident_r", [P, P], F32R)
        minus_half = sb("minus_half", [P, 1])
        zero_eps = sb("zero_eps", [P, 2])
        dft_scale = sb("dft_scale", [P, KC])
        bias_cols = sb("bias_cols", [P, 4 * KC])
        x_bn = sb("x_bn", [P, 6])
        x_mv = sb("x_mv", [P, Q, 2])
        x_ve = sb("x_ve", [P, Q, 1])
        x_rstd = sb("x_rstd", [P, Q, 1])
        h_bn = sb("h_bn", [P, 6])
        h_mv = sb("h_mv", [P, 2])
        h_ve = sb("h_ve", [P, 1])
        h_rstd = sb("h_rstd", [P, 1])
        x1_bn = sb("x1_bn", [P, 6])
        x1_mv = sb("x1_mv", [P, 2])
        x1_mean_ve = sb("x1_mean_ve", [P, TILES, 2])
        x1_rstd = sb("x1_rstd", [P, TILES, 1])
        x_res = sb("x_res", [P, 2, D])

        h_hi = [sb("h_hi0", [P, KC, NB], F32R)]
        h_lo = [sb("h_lo0", [P, KC, NB], F32R)]
        with ExitStack() as splitting:
            stage = [sb(f"stage{i}", [P, 4 * H], F32, splitting) for i in range(2)]
        h_hi.append(sb("h_hi1", [P, KC, NB], F32R))
        h_lo.append(sb("h_lo1", [P, KC, NB], F32R))
        c_state = sb("c_state", [P, KC, NB])
        xn_hi = sb("xn_hi", [P, KC, NB], F32R)
        xn_lo = sb("xn_lo", [P, KC, NB], F32R)
        gate_a = sb("gate_a", [P, NB])
        gate_b = sb("gate_b", [P, NB])
        gate_c = sb("gate_c", [P, NB])
        x_tile = sb("x_tile", [P, Q, D])
        ident_made_in = gate_c[:, 0:P]
        bias_rows = gate_c[0:4 * KC, P:2 * P]
        ident = ident_r[:].bitcast(F32)
        CREDIT = 1

        with ExitStack() as recurrence:
            w_hi = sb("w_hi", [P, KC, 4 * H], F32R, recurrence)
            w_lo = sb("w_lo", [P, KC, 4 * H], F32R, recurrence)
            with ExitStack() as making_m:
                t_hi = sb("t_hi", [P, KC, D], F32R, making_m)
                t_lo = sb("t_lo", [P, KC, D], F32R, making_m)
                wf_hi = sb("wf_hi", [P, KC, D], F32R, making_m)
                wf_lo = sb("wf_lo", [P, KC, D], F32R, making_m)
                g_hi = sb("g_hi", [P, KC, D], F32R, making_m)
                g_lo = sb("g_lo", [P, KC, D], F32R, making_m)
                raw = [[sb(f"raw{i}_{n}", [P, D], F32, making_m) for n in range(4)] for i in range(2)]
            u_hi = sb("u_hi", [P, KC, 4 * H], F32R, recurrence)
            u_lo = sb("u_lo", [P, KC, 4 * H], F32R, recurrence)
        m_hi = sb("m_hi", [P, KC, D], F32R)
        m_lo = sb("m_lo", [P, KC, D], F32R)
        ffn_bias_all = sb("ffn_bias_all", [P, D])
        RING = 8
        AHEAD = 5
        x1_tile = sb("x1_tile", [P, RING, D])
        xn2 = sb("xn2", [P, RING, D])
        xn2_hi = [sb(f"xn2_hi{i}", [P, KC, P], F32R) for i in range(2)]
        xn2_lo = [sb(f"xn2_lo{i}", [P, KC, P], F32R) for i in range(2)]
        y_tile = sb("y_tile", [P, RING, D])
        out_tile = sb("out_tile", [P, RING, D])
        y_bn = sb("y_bn", [P, 6])
        y_mv = sb("y_mv", [P, 2, 2])
        y_ve = sb("y_ve", [P, 2, 1])
        y_rstd = sb("y_rstd", [P, 2, 1])
        y_scaled_mean = sb("y_scaled_mean", [P, 1])
        y_centre = sb("y_centre", [P, 2, 1])

        consts_ready = sem("consts_ready")
        stats_seen = sem("stats_seen")
        ident_zeroed = sem("ident_zeroed")
        ident_made = sem("ident_made")
        ident_r_ready = sem("ident_r_ready")
        bias_loaded = sem("bias_loaded")
        bias_turned = sem("bias_turned")
        bias_ready = sem("bias_ready")
        edge_zeroed = sem("edge_zeroed")
        raw_loaded = [sem(f"raw_loaded{r}") for r in range(KC)]
        dft_hi_ready = sem("dft_hi_ready")
        dft_lo_ready = sem("dft_lo_ready")
        rows_folded = sem("rows_folded")
        cols_folded = sem("cols_folded")
        wf_hi_ready = sem("wf_hi_ready")
        wf_lo_ready = sem("wf_lo_ready")
        g_done = sem("g_done")
        g_hi_ready = sem("g_hi_ready")
        g_lo_ready = sem("g_lo_ready")
        m_done = sem("m_done")
        m_hi_ready = sem("m_hi_ready")
        m_lo_ready = sem("m_lo_ready")
        m_spilled = sem("m_spilled")
        stage_loaded = [sem(f"stage_loaded{i}") for i in range(2)]
        weight_hi_ready = sem("weight_hi_ready")
        weight_lo_ready = sem("weight_lo_ready")
        x_loaded = [sem(f"x_loaded{i}") for i in range(Q)]
        x_stat = sem("x_stat")
        x_rstd_ready = sem("x_rstd_ready")
        x_normed = sem("x_normed")
        x_turned = sem("x_turned")
        xn_hi_ready = sem("xn_hi_ready")
        xn_lo_ready = sem("xn_lo_ready")
        xn_used = sem("xn_used")
        gate_done = [sem(f"gate_done_{n}") for n in "icfo"]
        gate_read = [sem(f"gate_read_{n}") for n in "icfo"]
        ic_ready = sem("ic_ready")
        fc_ready = sem("fc_ready")
        c_ready = sem("c_ready")
        tanh_c_ready = sem("tanh_c_ready")
        h_ready = sem("h_ready")
        h_hi_ready = sem("h_hi_ready")
        h_lo_ready = sem("h_lo_ready")
        h_turned = sem("h_turned")
        h_stat = sem("h_stat")
        h_rstd_ready = sem("h_rstd_ready")
        h_normed = sem("h_normed")
        x_res_loaded = [sem(f"x_res_loaded{i}") for i in range(2)]
        x1_ready = sem("x1_ready")
        x1_stat = sem("x1_stat")
        x1_rstd_ready = sem("x1_rstd_ready")
        x1_stored = [sem(f"x1_stored{i}") for i in range(2)]
        m_loaded = sem("m_loaded")
        x1_loaded = [sem(f"x1_loaded{i}") for i in range(RING)]
        xn2_ready = sem("xn2_ready")
        xn2_turned = sem("xn2_turned")
        xn2_hi_ready = sem("xn2_hi_ready")
        xn2_lo_ready = sem("xn2_lo_ready")
        y_done = sem("y_done")
        y_ready = sem("y_ready")
        y_stat = sem("y_stat")
        y_rstd_ready = sem("y_rstd_ready")
        y_scaled_mean_ready = sem("y_scaled_mean_ready")
        y_centre_ready = sem("y_centre_ready")
        y_normed = sem("y_normed")
        out_ready = sem("out_ready")
        out_stored = [sem(f"out_stored{i}") for i in range(RING)]

        block = ctx.enter_context(nc.Block())

        def all_steps(eng, step):
            for blk in range(BLOCKS):
                step(blk, 0, 0)
                with eng.Fori(0, T // 2 - 1) as pair:
                    step(blk, 2 * pair + 1, 1)
                    step(blk, 2 * pair + 2, 0)
                step(blk, T - 1, 1)

        def number(blk, t):
            return t + blk * T

        def gates_of(t):
            kinds = [I, C, O] if isinstance(t, int) and t == 0 else [I, C, F, O]
            return [(j, kind) for j in range(KC) for kind in kinds]

        def uses(kind, blk, t, j):
            before = KC * number(blk, t) + j
            return before - KC * (blk + (0 if isinstance(t, int) and t == 0 else 1)) if kind == F else before

        def ffn_slots(eng, slot):
            for i in range(RING):
                slot(i, i)
            with eng.Fori(1, TILES // RING - 1) as g:
                for r in range(RING):
                    slot(g * RING + r, r)
            for i in range(TILES - RING, TILES):
                slot(i, i % RING)

        def in_slot(i):
            return i // 2 if isinstance(i, int) and i < 2 * Q and i % 2 == 0 else None

        def inside(i, ahead):
            return not isinstance(i, int) or i + ahead < TILES

        @block.sync
        def _(sp):
            def load_x(blk, t, q):
                at_least(sp, x_turned, Q * (number(blk, t) - 1) + q + 1)
                sp.dma_start(x_tile[:, q, :], x_rows[bass.ds(row(blk, t, q), P), :]).then_inc(x_loaded[q], 16)

            def load_residual(blk, t, q):
                sp.wait_ge(x1_stored[q % 2], 16 * (Q // 2 * number(blk, t) + q // 2 + CREDIT))
                sp.dma_start(x_res[:, q % 2, :], x_rows[bass.ds(row(blk, t, q), P), :]
                             ).then_inc(x_res_loaded[q % 2], 16)

            def store_x1(blk, t, q):
                sp.wait_ge(x1_stat, 3 * (Q * number(blk, t) + q) + 1)
                sp.dma_start(x1_rows[bass.ds(row(blk, t, q), P), :], x_res[:, q % 2, :]
                             ).then_inc(x1_stored[q % 2], 16)

            def load_weight_rows(rows, load):
                if load >= 2:
                    sp.wait_ge(dft_lo_ready, KC)
                at_least(sp, weight_lo_ready, 2 * (load - 2))
                sp.dma_start(stage[load % 2][:], rows).then_inc(stage_loaded[load % 2], 16)

            def load_spectral(r):
                a, b, c, d = raw[r % 2]
                k = P * (r % 2)
                first, second = (wf_real, wf_imag) if r < 2 else (wf_imag, wf_real)
                skip = 1 if k == 0 else 0
                mirror = (wf_real_reversed, wf_imag_reversed)
                for dst, src in ((a, first), (c, second)):
                    if r == 2:
                        sp.dma_start(dst[1:P, :], src[1:P, :]).then_inc(raw_loaded[r], 16)
                    else:
                        sp.dma_start(dst[:], src[k:k + P, :]).then_inc(raw_loaded[r], 16)
                for dst, src in ((b, mirror[first is wf_imag]), (d, mirror[second is wf_imag])):
                    sp.dma_start(dst[skip:P, :], src[k + skip - 1:k + P - 1, :]).then_inc(raw_loaded[r], 16)
                if r == 2:
                    sp.dma_start(a[0:1, :], wf_real[D // 2:D // 2 + 1, :]).then_inc(raw_loaded[r], 16)
                    sp.dma_start(d[0:1, :], wf_imag[D // 2:D // 2 + 1, :]).then_inc(raw_loaded[r], 16)

            sp.dma_start(bias_rows, gate_bias.rearrange("(c p) -> c p", p=P)).then_inc(bias_loaded, 16)
            for par in range(2):
                sp.sem_inc(x1_stored[par], 16 * CREDIT)
            load_spectral(0)
            sp.dma_start(stage[0][:].rearrange("p (k n) -> p k n", k=KC), dft.rearrange("(k p) n -> p k n", p=P)
                         ).then_inc(stage_loaded[0], 16)
            load_spectral(1)
            load_weight_rows(w_rows[0], 1)
            sp.wait_ge(cols_folded, 3 * 1)
            load_spectral(2)
            sp.wait_ge(cols_folded, 3 * 2)
            load_spectral(3)
            for q in range(Q):
                load_x(0, 0, q)
            for k in range(1, KC):
                load_weight_rows(w_rows[k], 1 + k)
            sp.wait_ge(m_lo_ready, KC)
            sp.dma_start(m_dram[0], wf_hi[:].rearrange("p k n -> p (k n)").bitcast(F32)).then_inc(m_spilled, 16)
            sp.dma_start(m_dram[1], wf_lo[:].rearrange("p k n -> p (k n)").bitcast(F32)).then_inc(m_spilled, 16)

            def step(blk, t, par):
                s0 = isinstance(t, int) and t == 0 and blk == 0
                last = isinstance(t, int) and t == T - 1 and blk == BLOCKS - 1
                for q in range(Q):
                    if not last:
                        load_x(*following(blk, t), q)
                    if s0:
                        load_weight_rows(u_rows[q], 1 + KC + q)
                if not s0:
                    load_residual(*preceding(blk, t), 0)
                    load_residual(*preceding(blk, t), 1)
                    for q in range(Q):
                        store_x1(*preceding(blk, t), q)
                        if q + 2 < Q:
                            load_residual(*preceding(blk, t), q + 2)

            all_steps(sp, step)

            load_residual(BLOCKS - 1, T - 1, 0)
            load_residual(BLOCKS - 1, T - 1, 1)
            sp.wait_ge(xn_used, STEPS - BLOCKS)
            sp.wait_ge(m_spilled, 32)

            def load_x1(i, r):
                at_least(sp, out_ready, i - (RING - 1))
                sp.dma_start(x1_tile[:, r, :], x1_rows[bass.ds(i * P, P), :]).then_inc(x1_loaded[r], 16)

            for par in range(2):
                sp.wait_ge(x1_stored[par], 16 * ((TILES - Q) // 2 + CREDIT))
            load_x1(0, 0)
            load_x1(1, 1)
            sp.dma_start(m_hi[:].rearrange("p k n -> p (k n)").bitcast(F32), m_dram[0]).then_inc(m_loaded, 16)
            sp.dma_start(m_lo[:].rearrange("p k n -> p (k n)").bitcast(F32), m_dram[1]).then_inc(m_loaded, 16)
            sp.dma_start(ffn_bias_all[:], ffn_bias.partition_broadcast(P)).then_inc(m_loaded, 16)
            for i in range(2, AHEAD):
                load_x1(i, i)

            def slot(i, r):
                if inside(i, AHEAD):
                    load_x1(i + AHEAD, (r + AHEAD) % RING)
                if in_slot(i) is not None:
                    store_x1(BLOCKS - 1, T - 1, in_slot(i))
                    if in_slot(i) + 2 < Q:
                        load_residual(BLOCKS - 1, T - 1, in_slot(i) + 2)
                    if in_slot(i) == Q - 1:
                        for par in range(2):
                            sp.wait_ge(x1_stored[par], 16 * (TILES // 2 + CREDIT))

            ffn_slots(sp, slot)

        @block.tensor
        def _(pe):
            def product(bank, lhs_hi, lhs_lo, rhs_hi, rhs_lo, start, stop):
                pe.matmul(bank, lhs_hi, rhs_hi, start=start, stop=False)
                pe.matmul(bank, lhs_hi, rhs_lo, start=False, stop=False)
                return pe.matmul(bank, lhs_lo, rhs_hi, start=False, stop=stop)

            def turn_x(blk, t, q):
                tile = Q * number(blk, t) + q
                pe.wait_ge(x_normed, tile + 1)
                for k in range(KC):
                    mm = pe.transpose(psum[:, 4 + q, k * P:(k + 1) * P], x_tile[:, q, k * P:(k + 1) * P],
                                      ident)
                mm.then_inc(x_turned, 1)

            def turn_h(blk, t, q, par, bank):
                pe.wait_ge(h_lo_ready, KC * number(blk, t) + KC)
                for k in range(KC):
                    for part in (h_hi, h_lo):
                        mm = pe.matmul(psum[:, bank, k * P:(k + 1) * P], part[par][:, k, q * P:(q + 1) * P],
                                       ident_r[:], start=(part is h_hi), stop=(part is h_lo))
                mm.then_inc(h_turned, 1)

            pe.wait_ge(ident_r_ready, 1)
            pe.wait_ge(bias_loaded, 16)
            pe.transpose(psum[:, 0, 0:4 * KC], bias_rows, ident_r[0:4 * KC, 0:4 * KC].bitcast(F32)
                         ).then_inc(bias_turned, 1)
            pe.wait_ge(bias_ready, 1)
            for r in range(KC):
                pe.wait_ge(dft_lo_ready, r + 1)
                pe.wait_ge(wf_lo_ready, r + 1)
                for jj in range(KC):
                    mm = product(psum[:, jj, :], wf_hi[:, r, jj * P:(jj + 1) * P], wf_lo[:, r, jj * P:(jj + 1) * P],
                                 t_hi[:, r, :], t_lo[:, r, :], r == 0, r == KC - 1)
                    if r == KC - 1:
                        mm.then_inc(g_done, 1)
            for q in range(Q):
                turn_x(0, 0, q)
            for dc in range(KC):
                for jj in range(KC):
                    if dc == 0:
                        pe.wait_ge(g_lo_ready, jj + 1)
                    mm = product(psum[:, dc, :], g_hi[:, jj, dc * P:(dc + 1) * P], g_lo[:, jj, dc * P:(dc + 1) * P],
                                 t_hi[:, jj, :], t_lo[:, jj, :], jj == 0, jj == KC - 1)
                mm.then_inc(m_done, 1)

            def turn_xn2(i, r):
                pe.wait_ge(xn2_ready, i + 1)
                at_least(pe, xn2_lo_ready, i - 1)
                for k in range(KC):
                    mm = pe.transpose(psum[:, r % 2, k * P:(k + 1) * P], xn2[:, r, k * P:(k + 1) * P], ident)
                mm.then_inc(xn2_turned, 1)

            def step(blk, t, par):
                s = number(blk, t)
                first = isinstance(t, int) and t == 0
                last = isinstance(t, int) and t == T - 1 and blk == BLOCKS - 1
                gates = gates_of(t)

                def x_part(j, kind):
                    pe.wait_ge(gate_read[kind], uses(kind, blk, t, j) + CREDIT)
                    col = COLUMN_OF_KIND[kind] * H + j * P
                    for k in range(KC):
                        mm = product(psum[:, kind, :], w_hi[:, k, col:col + P], w_lo[:, k, col:col + P],
                                     xn_hi[:, k, :], xn_lo[:, k, :], k == 0, first and k == KC - 1)
                    return mm

                def h_part(j, kind, fresh=False):
                    col = COLUMN_OF_KIND[kind] * H + j * P
                    for k in range(KC):
                        if fresh:
                            pe.wait_ge(h_lo_ready, KC * (s - 1) + k + 1)
                        mm = product(psum[:, kind, :], u_hi[:, k, col:col + P], u_lo[:, k, col:col + P],
                                     h_hi[1 - par][:, k, :], h_lo[1 - par][:, k, :], False, k == KC - 1)
                    mm.then_inc(gate_done[kind], 1)

                turn_h_after = {n: q for q, n in enumerate((1, 3, 5, 7) if first else (1, 4, 7, 9))}
                turn_x_after = {n: q for q, n in enumerate((2, 4, 8, 9) if first else (3, 6, 10, 12))}
                pe.wait_ge(xn_lo_ready, Q * s + Q)
                if first and blk == 0:
                    pe.wait_ge(m_lo_ready, KC)
                    pe.wait_ge(weight_lo_ready, 2 * KC)
                if not first and blk == 0 and par == 1:
                    pe.wait_ge(weight_lo_ready, 4 * KC)
                for n, (j, kind) in enumerate(gates[:-2]):
                    mm = x_part(j, kind)
                    if first:
                        mm.then_inc(gate_done[kind], 1)
                    else:
                        h_part(j, kind, fresh=(n == 0))
                    if n in turn_h_after and not (first and blk == 0):
                        q = turn_h_after[n]
                        tile = Q * number(*preceding(blk, t)) + q
                        pe.wait_ge(x1_ready, tile + CREDIT)
                        turn_h(*preceding(blk, t), q, 1 - par, 7)
                    if n in turn_x_after and not last:
                        q = turn_x_after[n]
                        if q == Q - 1 and not (first and blk == 0):
                            pe.wait_ge(x1_ready, Q * s + CREDIT)
                        turn_x(*following(blk, t), q)
                pending = gates[-2:]
                for j, kind in pending:
                    mm = x_part(j, kind)
                    if first:
                        mm.then_inc(gate_done[kind], 1)
                if not first:
                    mm.then_inc(xn_used, 1)
                    for j, kind in pending:
                        h_part(j, kind)
                        if last and kind == F:
                            pe.wait_ge(gate_read[I], uses(I, blk, t, j) + 1 + CREDIT)
                            turn_xn2(0, 0)

            all_steps(pe, step)

            for kind in (F, O):
                pe.wait_ge(gate_read[kind], uses(kind, BLOCKS - 1, T - 1, KC - 1) + 1 + CREDIT)
            pe.wait_ge(m_loaded, 48)

            def slot(i, r):
                if inside(i, 1):
                    turn_xn2(i + 1, (r + 1) % RING)
                if isinstance(i, int) and i == 0:
                    for q in range(Q):
                        turn_h(BLOCKS - 1, T - 1, q, 1, 4 + q)
                pe.wait_ge(xn2_lo_ready, i + 1)
                at_least(pe, y_ready, i - 1)
                hi, lo = xn2_hi[r % 2], xn2_lo[r % 2]
                for k in range(KC):
                    mm = product(psum[:, 2 + r % 2, :], hi[:, k, :], lo[:, k, :], m_hi[:, k, :], m_lo[:, k, :],
                                 k == 0, k == KC - 1)
                mm.then_inc(y_done, 1)

            ffn_slots(pe, slot)

        @block.scalar
        def _(act):
            for kind in (I, C, F, O):
                act.sem_inc(gate_read[kind], CREDIT)
            for r in range(RING):
                act.sem_inc(out_stored[r], 16 * CREDIT)
            act.wait_ge(bias_turned, 1)
            act.copy(bias_cols[:], psum[:, 0, 0:4 * KC]).then_inc(bias_ready, 1)
            def basis_hi(r):
                act.wait_ge(stage_loaded[0], 16)
                act.copy(t_hi[:, r, :], stage[0][:, r * D:(r + 1) * D]).then_inc(dft_hi_ready, 1)

            def folded_hi(r):
                act.wait_ge(cols_folded, 3 * (r + 1))
                act.copy(wf_hi[:, r, :], (gate_a, gate_b)[r % 2][:]).then_inc(wf_hi_ready, 1)

            def weight_hi(dst, k, load):
                act.wait_ge(stage_loaded[load % 2], 16 * (load // 2 + 1))
                for half in (slice(0, 2 * H), slice(2 * H, 4 * H)):
                    act.copy(dst[:, k, half], stage[load % 2][:, half]).then_inc(weight_hi_ready, 1)

            def input_hi(blk, t, q):
                act.wait_ge(x_turned, Q * number(blk, t) + q + 1)
                act.copy(xn_hi[:, :, q * P:(q + 1) * P], psum[:, 4 + q, :].rearrange("p (k n) -> p k n", k=KC)
                         ).then_inc(xn_hi_ready, 1)

            basis_hi(0)
            folded_hi(0)
            basis_hi(1)
            folded_hi(1)
            basis_hi(2)
            basis_hi(3)
            weight_hi(w_hi, 0, 1)
            folded_hi(2)
            folded_hi(3)
            act.wait_ge(consts_ready, 6)
            for jj in range(KC):
                act.wait_ge(g_done, jj + 1)
                act.activation(g_hi[:, jj, :], psum[:, jj, :], ACT.Copy, scale=dft_scale[:, jj:jj + 1]
                               ).then_inc(g_hi_ready, 1)
            for q in range(Q):
                input_hi(0, 0, q)
            weight_hi(w_hi, 1, 2)
            weight_hi(w_hi, 2, 3)
            weight_hi(w_hi, 3, 4)
            for dc in range(KC):
                act.wait_ge(m_done, dc + 1)
                act.copy(wf_hi[:, dc, :], psum[:, dc, :]).then_inc(m_hi_ready, 1)

            def step(blk, t, par):
                s = number(blk, t)
                first = isinstance(t, int) and t == 0
                last = isinstance(t, int) and t == T - 1 and blk == BLOCKS - 1

                def gate(j, kind, dst):
                    act.wait_ge(gate_done[kind], uses(kind, blk, t, j) + 1)
                    col = COLUMN_OF_KIND[kind] * KC + j
                    act.activation(dst[:], psum[:, kind, :], ACT.Tanh if kind == C else ACT.Sigmoid,
                                   bias=bias_cols[:, col:col + 1]).then_inc(gate_read[kind], 1)

                for j in range(KC):
                    n = KC * s + j
                    at_least(act, h_lo_ready, n)
                    gate(j, I, gate_a)
                    gate(j, C, gate_b)
                    if j == KC - 1 and not last:
                        if first:
                            act.wait_ge(gate_done[O], uses(O, blk, t, j) + 1)
                        else:
                            act.wait_ge(xn_used, s - blk)
                        for q in range(Q):
                            input_hi(*following(blk, t), q)
                    if not first:
                        gate(j, F, gate_c)
                    act.wait_ge(c_ready, n + 1)
                    act.activation(gate_b[:], c_state[:, j, :], ACT.Tanh).then_inc(tanh_c_ready, 1)
                    gate(j, O, gate_c)
                    act.wait_ge(h_ready, n + 1)
                    act.copy(h_hi[par][:, j, :], gate_a[:]).then_inc(h_hi_ready, 1)
                    if first and blk == 0:
                        if j == 0:
                            act.wait_ge(m_spilled, 32)
                        weight_hi(u_hi, j, 1 + KC + j)

            all_steps(act, step)

            def store_out(i, r):
                act.wait_ge(out_ready, i + 1)
                act.dma_start(out_rows[bass.ds(i * P, P), :], out_tile[:, r, :]).then_inc(out_stored[r], 16)

            def y_norm(i, r):
                act.wait_ge(y_centre_ready, i + 1)
                act.activation(y_tile[:, r, :], y_tile[:, r, :], ACT.Identity, bias=y_centre[:, r % 2, :],
                               scale=y_rstd[:, r % 2, :]).then_inc(y_normed, 1)

            def slot(i, r):
                if inside(i, 1):
                    xn2_part(i + 1, r + 1)
                if not (isinstance(i, int) and i == 0):
                    y_norm(i - 1, (r - 1) % RING)
                if not (isinstance(i, int) and i < 2):
                    store_out(i - 2, (r - 2) % RING)

            def xn2_part(i, r):
                act.wait_ge(xn2_turned, i + 1)
                at_least(act, y_done, i - 1)
                act.copy(xn2_hi[r % 2][:].rearrange("p k n -> p (k n)"), psum[:, r % 2, :]
                         ).then_inc(xn2_hi_ready, 1)

            xn2_part(0, 0)
            ffn_slots(act, slot)
            y_norm(TILES - 1, (TILES - 1) % RING)
            for i in (TILES - 2, TILES - 1):
                store_out(i, i % RING)
            for r in range(RING):
                act.wait_ge(out_stored[r], 16 * (TILES // RING + CREDIT))

        @block.vector
        def _(dve):
            dve.sem_inc(x1_ready, CREDIT)
            dve.wait_ge(ident_made, 1)
            dve.tensor_copy(ident_r[:], ident_made_in).then_inc(ident_r_ready, 1)
            dve.wait_ge(consts_ready, 6)

            def norm_x(blk, t, q):
                tile = Q * number(blk, t) + q
                b = q
                dve.wait_ge(x_loaded[b], 16 * (number(blk, t) + 1))
                dve.bn_stats(x_bn[:], x_tile[:, b, :]).then_inc(x_stat, 1)
                dve.wait_ge(x_stat, 3 * tile + 1)
                dve.sem_inc(stats_seen, 1)
                dve.bn_aggr(x_mv[:, b, :], x_bn[:]).then_inc(x_stat, 1)
                dve.wait_ge(x_stat, 3 * tile + 2)
                dve.tensor_scalar_add(x_ve[:, b, :], x_mv[:, b, 1:2], EPS).then_inc(x_stat, 1)
                dve.wait_ge(x_rstd_ready, tile + 1)
                dve.tensor_scalar(x_tile[:, b, :], x_tile[:, b, :], x_mv[:, b, 0:1], x_rstd[:, b, :],
                                  ALU.subtract, ALU.mult).then_inc(x_normed, 1)

            def input_lo(blk, t, q):
                dve.wait_ge(xn_hi_ready, Q * number(blk, t) + q + 1)
                part = (slice(None), slice(None), slice(q * P, (q + 1) * P))
                dve.tensor_sub(xn_lo[part], psum[:, 4 + q, :].rearrange("p (k n) -> p k n", k=KC),
                               xn_hi[part].bitcast(F32)).then_inc(xn_lo_ready, 1)

            def fold(r):
                a, b, c, d = raw[r % 2]
                op = ALU.add if r < 2 else ALU.subtract
                dve.wait_ge(raw_loaded[r], 16 * (6 if r == 2 else 4))
                dve.wait_ge(edge_zeroed, 3 if r == 2 else 2)
                dve.tensor_tensor(a[:], a[:], b[:], op).then_inc(rows_folded, 1)
                dve.tensor_tensor(c[:], d[:], c[:], op).then_inc(rows_folded, 1)
                dve.wait_ge(rows_folded, 2 * r + 2)
                at_least(dve, wf_lo_ready, r - 1)
                f = (gate_a, gate_b)[r % 2]
                half = D // 2
                dve.tensor_copy(f[:, 0:D:half], a[:, 0:D:half]).then_inc(cols_folded, 1)
                dve.tensor_tensor(f[:, 1:half], a[:, 1:half], a[:, D - 1:half:-1], ALU.add).then_inc(cols_folded, 1)
                dve.tensor_tensor(f[:, half + 1:D], c[:, 1:half], c[:, D - 1:half:-1], ALU.subtract
                                  ).then_inc(cols_folded, 1)

            def folded_lo(r):
                dve.wait_ge(wf_hi_ready, r + 1)
                dve.tensor_sub(wf_lo[:, r, :], (gate_a, gate_b)[r % 2][:], wf_hi[:, r, :].bitcast(F32)
                               ).then_inc(wf_lo_ready, 1)

            def weight_lo(dst_hi, dst, k, load):
                for n, half in enumerate((slice(0, 2 * H), slice(2 * H, 4 * H))):
                    dve.wait_ge(weight_hi_ready, 2 * (load - 1) + n + 1)
                    dve.tensor_sub(dst[:, k, half], stage[load % 2][:, half], dst_hi[:, k, half].bitcast(F32)
                                   ).then_inc(weight_lo_ready, 1)

            def basis_lo(r):
                dve.wait_ge(dft_hi_ready, r + 1)
                dve.tensor_sub(t_lo[:, r, :], stage[0][:, r * D:(r + 1) * D], t_hi[:, r, :].bitcast(F32)
                               ).then_inc(dft_lo_ready, 1)

            fold(0)
            basis_lo(0)
            folded_lo(0)
            fold(1)
            basis_lo(1)
            folded_lo(1)
            basis_lo(2)
            basis_lo(3)
            weight_lo(w_hi, w_lo, 0, 1)
            fold(2)
            folded_lo(2)
            fold(3)
            folded_lo(3)
            for q in range(Q):
                norm_x(0, 0, q)
            for jj in range(KC):
                dve.wait_ge(g_hi_ready, jj + 1)
                dve.scalar_tensor_tensor(out=g_lo[:, jj, :], in0=psum[:, jj, :], scalar=dft_scale[:, jj:jj + 1],
                                         in1=g_hi[:, jj, :].bitcast(F32), op0=ALU.mult, op1=ALU.subtract
                                         ).then_inc(g_lo_ready, 1)
            for q in range(Q):
                input_lo(0, 0, q)
            weight_lo(w_hi, w_lo, 1, 2)
            weight_lo(w_hi, w_lo, 2, 3)
            weight_lo(w_hi, w_lo, 3, 4)
            for dc in range(KC):
                dve.wait_ge(m_hi_ready, dc + 1)
                dve.tensor_sub(wf_lo[:, dc, :], psum[:, dc, :], wf_hi[:, dc, :].bitcast(F32)).then_inc(m_lo_ready, 1)

            def h_statistics(blk, t, q, bank):
                tile = Q * number(blk, t) + q
                dve.wait_ge(h_turned, tile + 1)
                dve.bn_stats(h_bn[:], psum[:, bank, :]).then_inc(h_stat, 1)
                dve.wait_ge(h_stat, 3 * tile + 1)
                dve.sem_inc(stats_seen, 1)
                dve.bn_aggr(h_mv[:], h_bn[:]).then_inc(h_stat, 1)
                dve.wait_ge(h_stat, 3 * tile + 2)
                dve.tensor_scalar_add(h_ve[:], h_mv[:, 1:2], EPS).then_inc(h_stat, 1)

            def residual(blk, t, q, bank):
                h_statistics(blk, t, q, bank)
                x1_and_statistics(blk, t, q, bank)

            def x1_and_statistics(blk, t, q, bank):
                tile = Q * number(blk, t) + q
                b = q % 2
                dve.wait_ge(h_rstd_ready, tile + 1)
                dve.tensor_scalar(psum[:, bank, :], psum[:, bank, :], h_mv[:, 0:1], h_rstd[:],
                                  ALU.subtract, ALU.mult).then_inc(h_normed, 1)
                dve.wait_ge(h_normed, tile + 1)
                dve.wait_ge(x_res_loaded[b], 16 * (Q // 2 * number(blk, t) + q // 2 + 1))
                dve.tensor_tensor(x_res[:, b, :], psum[:, bank, :], x_res[:, b, :], ALU.add).then_inc(x1_ready, 1)
                dve.wait_ge(x1_ready, tile + 1 + CREDIT)
                dve.bn_stats(x1_bn[:], x_res[:, b, :]).then_inc(x1_stat, 1)
                dve.wait_ge(x1_stat, 3 * tile + 1)
                dve.sem_inc(stats_seen, 1)
                dve.bn_aggr(x1_mv[:], x1_bn[:]).then_inc(x1_stat, 1)
                dve.wait_ge(x1_stat, 3 * tile + 2)
                at = t * (B // P) + (blk * Q + q)
                dve.tensor_tensor(x1_mean_ve[:, bass.ds(at, 1), :].rearrange("p a b -> p (a b)"), x1_mv[:],
                                  zero_eps[:], ALU.add).then_inc(x1_stat, 1)

            def norm_x1(i, r):
                dve.wait_ge(x1_loaded[r], 16 // RING * (i - r) + 16)
                at_least(dve, xn2_turned, i - (RING - 1))
                if isinstance(i, int) and i == 0:
                    dve.wait_ge(x1_rstd_ready, TILES - Q)
                dve.tensor_scalar(xn2[:, r, :], x1_tile[:, r, :],
                                  x1_mean_ve[:, bass.ds(i, 1), 0:1].rearrange("p a b -> p (a b)"),
                                  x1_rstd[:, bass.ds(i, 1), :].rearrange("p a b -> p (a b)"),
                                  ALU.subtract, ALU.mult).then_inc(xn2_ready, 1)

            def step(blk, t, par):
                s = number(blk, t)
                first = isinstance(t, int) and t == 0
                start = first and blk == 0
                last = isinstance(t, int) and t == T - 1 and blk == BLOCKS - 1
                for j in range(KC):
                    n = KC * s + j
                    if not last and j == 0:
                        norm_x(*following(blk, t), 0)
                    dve.wait_ge(gate_read[I], n + 1 + CREDIT)
                    dve.wait_ge(gate_read[C], n + 1 + CREDIT)
                    if first:
                        dve.tensor_mul(c_state[:, j, :], gate_a[:], gate_b[:]).then_inc(c_ready, 1)
                    else:
                        dve.tensor_mul(gate_a[:], gate_a[:], gate_b[:]).then_inc(ic_ready, 1)
                    if not start and j < 3:
                        residual(*preceding(blk, t), (0, 1, 3)[j], 7)
                    if not last and j < 3:
                        norm_x(*following(blk, t), j + 1)
                    if last and j == 3:
                        norm_x1(0, 0)
                        norm_x1(1, 1)
                    if j == KC - 1 and not last:
                        for q in range(Q):
                            input_lo(*following(blk, t), q)
                    if not first:
                        done = uses(F, blk, t, j) + 1
                        dve.wait_ge(gate_read[F], done + CREDIT)
                        dve.tensor_mul(gate_c[:], gate_c[:], c_state[:, j, :]).then_inc(fc_ready, 1)
                        dve.wait_ge(fc_ready, done)
                        dve.wait_ge(ic_ready, done)
                        dve.tensor_add(c_state[:, j, :], gate_c[:], gate_a[:]).then_inc(c_ready, 1)
                    dve.wait_ge(tanh_c_ready, n + 1)
                    dve.wait_ge(gate_read[O], n + 1 + CREDIT)
                    dve.tensor_mul(gate_a[:], gate_b[:], gate_c[:]).then_inc(h_ready, 1)
                    dve.wait_ge(h_hi_ready, n + 1)
                    dve.tensor_sub(h_lo[par][:, j, :], gate_a[:], h_hi[par][:, j, :].bitcast(F32)
                                   ).then_inc(h_lo_ready, 1)
                    if not start and j == 1:
                        residual(*preceding(blk, t), 2, 7)
                    if start:
                        weight_lo(u_hi, u_lo, j, 1 + KC + j)

            all_steps(dve, step)

            def lo_xn2(i, r):
                dve.wait_ge(xn2_hi_ready, i + 1)
                dve.tensor_sub(xn2_lo[r % 2][:].rearrange("p k n -> p (k n)"), psum[:, r % 2, :],
                               xn2_hi[r % 2][:].rearrange("p k n -> p (k n)").bitcast(F32)).then_inc(xn2_lo_ready, 1)

            lo_xn2(0, 0)
            dve.wait_ge(m_loaded, 48)

            def slot(i, r):
                if inside(i, 2):
                    norm_x1(i + 2, (r + 2) % RING)
                if inside(i, 1):
                    lo_xn2(i + 1, (r + 1) % RING)
                if in_slot(i) is not None:
                    h_statistics(BLOCKS - 1, T - 1, in_slot(i), 4 + in_slot(i))
                b = r % 2
                dve.wait_ge(y_done, i + 1)
                at_least(dve, out_ready, i - (RING - 1))
                dve.tensor_add(y_tile[:, r, :], psum[:, 2 + b, :], ffn_bias_all[:]).then_inc(y_ready, 1)
                dve.wait_ge(y_ready, i + 1)
                dve.bn_stats(y_bn[:], y_tile[:, r, :]).then_inc(y_stat, 1)
                at_least(dve, y_centre_ready, i - 1)
                dve.wait_ge(y_stat, 3 * i + 1)
                dve.sem_inc(stats_seen, 1)
                dve.bn_aggr(y_mv[:, b, :], y_bn[:]).then_inc(y_stat, 1)
                dve.wait_ge(y_stat, 3 * i + 2)
                dve.tensor_scalar_add(y_ve[:, b, :], y_mv[:, b, 1:2], EPS).then_inc(y_stat, 1)
                if in_slot(i) is not None:
                    x1_and_statistics(BLOCKS - 1, T - 1, in_slot(i), 4 + in_slot(i))
                if isinstance(i, int) and i == 2 * Q - 1:
                    dve.wait_ge(x1_rstd_ready, TILES)

            ffn_slots(dve, slot)

        @block.gpsimd
        def _(pool):
            pool.memset(ident_made_in, 0.0).then_inc(ident_zeroed, 1)
            pool.wait_ge(ident_zeroed, 1)
            pool.affine_select(out=ident_made_in, in_=ident_made_in, compare_op=ALU.not_equal, fill=1.0, base=0,
                               pattern=[[-1, P]], channel_multiplier=1).then_inc(ident_made, 1)
            pool.memset(minus_half[:], -0.5).then_inc(consts_ready, 1)
            pool.wait_ge(consts_ready, 1)
            pool.memset(zero_eps[:, 0:1], 0.0).then_inc(consts_ready, 1)
            pool.memset(zero_eps[:, 1:2], EPS).then_inc(consts_ready, 1)
            pool.memset(dft_scale[:, 0:KC // 2], 1.0 / D).then_inc(consts_ready, 1)
            pool.memset(dft_scale[:, KC // 2:KC], -1.0 / D).then_inc(consts_ready, 1)
            pool.wait_ge(consts_ready, 5)
            pool.memset(dft_scale[0:1, KC // 2:KC // 2 + 1], 1.0 / D).then_inc(consts_ready, 1)
            pool.memset(raw[0][1][0:1, :], 0.0).then_inc(edge_zeroed, 1)
            pool.memset(raw[0][3][0:1, :], 0.0).then_inc(edge_zeroed, 1)

            def rstd_x(blk, t, q):
                tile = Q * number(blk, t) + q
                pool.wait_ge(x_stat, 3 * tile + 3)
                pool.tensor_tensor(x_rstd[:, q, :], x_ve[:, q, :], minus_half[:], ALU.pow
                                   ).then_inc(x_rstd_ready, 1)

            def rstd_residual(blk, t, q):
                tile = Q * number(blk, t) + q
                pool.wait_ge(h_stat, 3 * tile + 3)
                pool.tensor_tensor(h_rstd[:], h_ve[:], minus_half[:], ALU.pow).then_inc(h_rstd_ready, 1)
                pool.wait_ge(x1_stat, 3 * tile + 3)
                at = t * (B // P) + (blk * Q + q)
                pool.tensor_tensor(x1_rstd[:, bass.ds(at, 1), :].rearrange("p a b -> p (a b)"),
                                   x1_mean_ve[:, bass.ds(at, 1), 1:2].rearrange("p a b -> p (a b)"),
                                   minus_half[:], ALU.pow).then_inc(x1_rstd_ready, 1)

            pool.wait_ge(cols_folded, 3)
            pool.memset(raw[0][2][0:1, :], 0.0).then_inc(edge_zeroed, 1)
            for q in range(Q):
                rstd_x(0, 0, q)

            def step(blk, t, par):
                start = isinstance(t, int) and t == 0 and blk == 0
                last = isinstance(t, int) and t == T - 1 and blk == BLOCKS - 1
                for j in range(KC):
                    if not last and j == 0:
                        rstd_x(*following(blk, t), 0)
                    if not start and j < 3:
                        rstd_residual(*preceding(blk, t), (0, 1, 3)[j])
                    if not last and j < 3:
                        rstd_x(*following(blk, t), j + 1)
                    if not start and j == 1:
                        rstd_residual(*preceding(blk, t), 2)

            all_steps(pool, step)

            def add_up(i, r):
                pool.wait_ge(y_normed, i + 1)
                pool.wait_ge(out_stored[r], 16 // RING * (i - r) + 16 * CREDIT)
                pool.tensor_tensor(out_tile[:, r, :], y_tile[:, r, :], x1_tile[:, r, :], ALU.add
                                   ).then_inc(out_ready, 1)

            def slot(i, r):
                if in_slot(i) is not None:
                    rstd_residual(BLOCKS - 1, T - 1, in_slot(i))
                pool.wait_ge(y_stat, 3 * i + 3)
                at_least(pool, y_normed, i - 1)
                pool.tensor_tensor(y_rstd[:, r % 2, :], y_ve[:, r % 2, :], minus_half[:], ALU.pow
                                   ).then_inc(y_rstd_ready, 1)
                pool.wait_ge(y_rstd_ready, i + 1)
                pool.tensor_tensor(y_scaled_mean[:], y_mv[:, r % 2, 0:1], y_rstd[:, r % 2, :], ALU.mult
                                   ).then_inc(y_scaled_mean_ready, 1)
                pool.wait_ge(y_scaled_mean_ready, i + 1)
                pool.tensor_tensor(y_centre[:, r % 2, :], zero_eps[:, 0:1], y_scaled_mean[:], ALU.subtract
                                   ).then_inc(y_centre_ready, 1)
                if not (isinstance(i, int) and i == 0):
                    add_up(i - 1, (r - 1) % RING)

            ffn_slots(pool, slot)
            add_up(TILES - 1, (TILES - 1) % RING)


_INS = ["L0_attn_input_seq", "L0_attn_w", "L0_attn_u", "L0_attn_bias",
        "L0_ffn_w_freq_real", "L0_ffn_w_freq_imag", "L0_ffn_bias"]


def _real_fourier_basis(n):
    import numpy as np

    kd = np.outer(np.arange(n // 2 + 1), np.arange(n)) % n
    angle = 2.0 * np.pi * kd / n
    return np.concatenate([np.cos(angle), np.sin(angle[1:n // 2])]).astype(np.float32)


def kernel(**inputs):
    import numpy as _np
    import concourse.bacc as _bacc
    from concourse import mybir as _mybir
    from concourse.bass_utils import run_bass_kernel_spmd as _run

    nc = _bacc.Bacc("TRN2", target_bir_lowering=False, num_devices=1)
    arrays, args = {}, []
    for name in _INS:
        a = _np.ascontiguousarray(inputs[name])
        arrays[f"in_{name}_dram"] = a
        args.append(nc.dram_tensor(f"in_{name}_dram", a.shape, _mybir.dt.from_np(a.dtype), kind="ExternalInput").ap())
    for name in ("L0_ffn_w_freq_real", "L0_ffn_w_freq_imag"):
        a = _np.ascontiguousarray(inputs[name][::-1])
        arrays[f"in_{name}_reversed_dram"] = a
        args.append(nc.dram_tensor(f"in_{name}_reversed_dram", a.shape, _mybir.dt.from_np(a.dtype),
                                   kind="ExternalInput").ap())
    basis = _real_fourier_basis(inputs["L0_ffn_w_freq_real"].shape[0])
    arrays["fourier_basis_dram"] = basis
    args.append(nc.dram_tensor("fourier_basis_dram", basis.shape, _mybir.dt.float32, kind="ExternalInput").ap())
    shape = tuple(inputs["L0_attn_input_seq"].shape)
    args.append(nc.dram_tensor("out_0_dram", shape, _mybir.dt.float32, kind="ExternalOutput").ap())
    build(nc, *args)
    r = _run(nc, [arrays], core_ids=[0])
    return r.results[0]["out_0_dram"]
```

```python
from contextlib import ExitStack

import concourse.bass as bass
from concourse import mybir

P = 128
F32 = mybir.dt.float32
F32R = mybir.dt.float32r
ALU = mybir.AluOpType
ACT = mybir.ActivationFunctionType

I, C, F, O = range(4)
COLUMN_OF_KIND = {I: 0, F: 1, O: 2, C: 3}
EPS = 1e-5


def at_least(eng, sem, value):
    if isinstance(value, int) and value <= 0:
        return
    eng.wait_ge(sem, value)


def build(nc, x, w, u, gate_bias, wf_real, wf_imag, ffn_bias, wf_real_reversed,
          wf_imag_reversed, dft, out):
    T, B, D = x.shape
    H = u.shape[0]
    KC = D // P
    NB = 512
    BLOCKS = B // NB
    Q = NB // P
    STEPS = T * BLOCKS
    TILES = STEPS * Q
    assert D == H == 512 and w.shape[1] == 4 * H and B % NB == 0 and T % 2 == 0

    x_rows = x.rearrange("t b d -> (t b) d")
    out_rows = out.rearrange("t b d -> (t b) d")
    w_rows = w.rearrange("(k p) n -> k p n", p=P)
    u_rows = u.rearrange("(k p) n -> k p n", p=P)
    x1_rows = nc.dram_tensor("x1_scratch", (T * B, D), F32, kind="Internal").ap()
    m_dram = nc.dram_tensor("m_scratch", (2, P, KC * D), F32, kind="Internal").ap()

    def row(blk, t, q):
        return t * B + (blk * NB + q * P)

    def following(blk, t):
        return (blk + 1, 0) if isinstance(t, int) and t == T - 1 else (blk, t + 1)

    def preceding(blk, t):
        return (blk - 1, T - 1) if isinstance(t, int) and t == 0 else (blk, t - 1)

    with ExitStack() as ctx:
        def sb(name, shape, dt=F32, where=ctx):
            return where.enter_context(nc.sbuf_tensor(name, shape, dt))

        def sem(name):
            return ctx.enter_context(nc.semaphore(name))

        psum = ctx.enter_context(nc.psum_tensor("psum", [P, 8, 512], F32))

        ident_r = sb("ident_r", [P, P], F32R)
        minus_half = sb("minus_half", [P, 1])
        zero = sb("zero", [P, 1])
        dft_scale = sb("dft_scale", [P, KC])
        bias_cols = sb("bias_cols", [P, 4 * KC])
        x_bn = sb("x_bn", [P, 6])
        x_mv = sb("x_mv", [P, Q, 2])
        x_ve = sb("x_ve", [P, Q, 1])
        x_rstd = sb("x_rstd", [P, Q, 1])
        h_bn = sb("h_bn", [P, 6])
        h_mv = sb("h_mv", [P, 2])
        h_ve = sb("h_ve", [P, 1])
        h_rstd = sb("h_rstd", [P, 1])
        x1_bn = sb("x1_bn", [P, 6])
        x1_mv = sb("x1_mv", [P, 2])
        x1_ve = sb("x1_ve", [P, 1])
        x1_rstd = sb("x1_rstd", [P, TILES, 1])
        x1_scaled_mean = sb("x1_scaled_mean", [P, 1])
        x1_centre = sb("x1_centre", [P, TILES, 1])
        x_res = sb("x_res", [P, 2, D])

        with ExitStack() as before_first_h:
            stage_in_h0 = sb("stage_in_h0", [P, 4 * H], F32, before_first_h)
        h_hi = [sb("h_hi0", [P, KC, NB], F32R)]
        h_lo = [sb("h_lo0", [P, KC, NB], F32R)]
        with ExitStack() as before_second_h:
            stage = [sb(f"stage{i}", [P, 4 * H], F32, before_second_h) for i in range(2)]
        h_hi.append(sb("h_hi1", [P, KC, NB], F32R))
        h_lo.append(sb("h_lo1", [P, KC, NB], F32R))
        c_state = sb("c_state", [P, KC, NB])
        h_full = sb("h_full", [P, KC, NB])
        xn_hi = sb("xn_hi", [P, KC, NB], F32R)
        xn_lo = sb("xn_lo", [P, KC, NB], F32R)
        stage_in_c = c_state[:].rearrange("p k n -> p (k n)")
        STAGE_OF_LOAD = (0, 1, 0, 2, 3, 0, 1, 0, 1)
        stages = (stage[0][:], stage[1][:], stage_in_c, stage_in_h0[:])

        def loads_into(load):
            place = STAGE_OF_LOAD[load]
            return place, STAGE_OF_LOAD[1:load + 1].count(place)

        gate_a = sb("gate_a", [P, NB])
        gate_b = sb("gate_b", [P, NB])
        gate_c = sb("gate_c", [P, NB])
        X_SLOTS = 2
        x_tile = sb("x_tile", [P, X_SLOTS, D])
        ident_made_in = gate_c[:, 0:P]
        bias_rows = gate_c[0:4 * KC, P:2 * P]
        ident = ident_r[:].bitcast(F32)
        TILE_BANK = 4
        XN2_BANK = 4
        Y_BANK = 6
        CREDIT = 1

        with ExitStack() as recurrence:
            w_hi = sb("w_hi", [P, KC, 4 * H], F32R, recurrence)
            w_lo = sb("w_lo", [P, KC, 4 * H], F32R, recurrence)
            with ExitStack() as making_m:
                t_hi = sb("t_hi", [P, KC, D], F32R, making_m)
                t_lo = sb("t_lo", [P, KC, D], F32R, making_m)
                wf_hi = sb("wf_hi", [P, KC, D], F32R, making_m)
                wf_lo = sb("wf_lo", [P, KC, D], F32R, making_m)
                g_hi = sb("g_hi", [P, KC, D], F32R, making_m)
                g_lo = sb("g_lo", [P, KC, D], F32R, making_m)
                raw = [[sb(f"raw{i}_{n}", [P, D], F32, making_m) for n in range(4)] for i in range(2)]
            u_hi = sb("u_hi", [P, KC, 4 * H], F32R, recurrence)
            u_lo = sb("u_lo", [P, KC, 4 * H], F32R, recurrence)
        m_hi = sb("m_hi", [P, KC, D], F32R)
        m_lo = sb("m_lo", [P, KC, D], F32R)
        ffn_bias_all = sb("ffn_bias_all", [P, D])
        RING = 8
        AHEAD = 5
        x1_tile = sb("x1_tile", [P, RING, D])
        xn2 = sb("xn2", [P, RING, D])
        xn2_hi = [sb(f"xn2_hi{i}", [P, KC, P], F32R) for i in range(2)]
        xn2_lo = [sb(f"xn2_lo{i}", [P, KC, P], F32R) for i in range(2)]
        y_tile = sb("y_tile", [P, RING, D])
        out_tile = sb("out_tile", [P, RING, D])
        y_bn = sb("y_bn", [P, 6])
        y_mv = sb("y_mv", [P, 2, 2])
        y_ve = sb("y_ve", [P, 2, 1])
        y_rstd = sb("y_rstd", [P, 2, 1])
        y_scaled_mean = sb("y_scaled_mean", [P, 1])
        y_centre = sb("y_centre", [P, 2, 1])

        stats_seen = sem("stats_seen")
        rstd_seen = sem("rstd_seen")
        consts_ready = sem("consts_ready")
        ident_zeroed = sem("ident_zeroed")
        ident_made = sem("ident_made")
        ident_r_ready = sem("ident_r_ready")
        bias_loaded = sem("bias_loaded")
        bias_turned = sem("bias_turned")
        bias_ready = sem("bias_ready")
        edge_zeroed = sem("edge_zeroed")
        raw_loaded = [sem(f"raw_loaded{r}") for r in range(KC)]
        basis_loaded = [sem(f"basis_loaded{r}") for r in range(KC)]
        dft_hi_ready = sem("dft_hi_ready")
        dft_lo_ready = sem("dft_lo_ready")
        rows_folded = sem("rows_folded")
        cols_folded = sem("cols_folded")
        wf_hi_ready = sem("wf_hi_ready")
        wf_lo_ready = sem("wf_lo_ready")
        g_done = sem("g_done")
        g_hi_ready = sem("g_hi_ready")
        g_lo_ready = sem("g_lo_ready")
        m_done = sem("m_done")
        m_hi_ready = sem("m_hi_ready")
        m_lo_ready = sem("m_lo_ready")
        m_spilled = sem("m_spilled")
        stage_loaded = [sem(f"stage_loaded{i}") for i in range(4)]
        weight_hi_ready = sem("weight_hi_ready")
        weight_lo_ready = sem("weight_lo_ready")
        weight_lo_by_pool = sem("weight_lo_by_pool")
        first_x_loaded = [sem(f"first_x_loaded{i}") for i in range(Q)]
        x_loaded = [sem(f"x_loaded{i}") for i in range(X_SLOTS)]
        x_stat = sem("x_stat")
        x_rstd_ready = sem("x_rstd_ready")
        x_normed = sem("x_normed")
        x_turned = sem("x_turned")
        xn_hi_ready = sem("xn_hi_ready")
        xn_lo_ready = sem("xn_lo_ready")
        xn_used = sem("xn_used")
        gate_done = [sem(f"gate_done_{n}") for n in "icfo"]
        gate_read = [sem(f"gate_read_{n}") for n in "icfo"]
        ic_ready = sem("ic_ready")
        fc_ready = sem("fc_ready")
        c_ready = sem("c_ready")
        tanh_c_ready = sem("tanh_c_ready")
        h_ready = sem("h_ready")
        h_hi_ready = sem("h_hi_ready")
        h_lo_ready = sem("h_lo_ready")
        h_turned = sem("h_turned")
        h_stat = sem("h_stat")
        h_rstd_ready = sem("h_rstd_ready")
        h_normed = sem("h_normed")
        x_res_loaded = [sem(f"x_res_loaded{i}") for i in range(2)]
        x1_ready = sem("x1_ready")
        x1_stat = sem("x1_stat")
        x1_rstd_ready = sem("x1_rstd_ready")
        x1_scaled_mean_ready = sem("x1_scaled_mean_ready")
        x1_centre_ready = sem("x1_centre_ready")
        x1_stored = [sem(f"x1_stored{i}") for i in range(2)]
        m_loaded = [sem(f"m_loaded{k}") for k in range(KC)]
        ffn_bias_loaded = sem("ffn_bias_loaded")
        x1_loaded = [sem(f"x1_loaded{i}") for i in range(RING)]
        xn2_ready = sem("xn2_ready")
        xn2_turned = sem("xn2_turned")
        xn2_hi_ready = sem("xn2_hi_ready")
        xn2_lo_ready = sem("xn2_lo_ready")
        y_done = sem("y_done")
        y_ready = sem("y_ready")
        y_stat = sem("y_stat")
        y_rstd_ready = sem("y_rstd_ready")
        y_scaled_mean_ready = sem("y_scaled_mean_ready")
        y_centre_ready = sem("y_centre_ready")
        y_normed = sem("y_normed")
        out_ready = sem("out_ready")
        out_stored = [sem(f"out_stored{i}") for i in range(RING)]

        block = ctx.enter_context(nc.Block())

        def all_steps(eng, step):
            for blk in range(BLOCKS):
                step(blk, 0, 0)
                with eng.Fori(0, T // 2 - 1) as pair:
                    step(blk, 2 * pair + 1, 1)
                    step(blk, 2 * pair + 2, 0)
                step(blk, T - 1, 1)

        def number(blk, t):
            return t + blk * T

        def is_start(blk, t):
            return blk == 0 and isinstance(t, int) and t == 0

        def is_last(blk, t):
            return blk == BLOCKS - 1 and isinstance(t, int) and t == T - 1

        def gates_of(t):
            kinds = [I, C, O] if isinstance(t, int) and t == 0 else [I, C, F, O]
            return [(j, kind) for j in range(KC) for kind in kinds]

        def uses(kind, blk, t, j):
            before = KC * number(blk, t) + j
            return before - KC * (blk + (0 if isinstance(t, int) and t == 0 else 1)) if kind == F else before

        def x_place(blk, t, q):
            return h_full[:, q, :] if is_start(blk, t) else x_tile[:, q % X_SLOTS, :]

        def x_is_loaded(eng, blk, t, q):
            if is_start(blk, t):
                eng.wait_ge(first_x_loaded[q], 16)
            else:
                slot, uses_of_slot = q % X_SLOTS, Q // X_SLOTS * (number(blk, t) - 1) + q // X_SLOTS + 1
                eng.wait_ge(x_loaded[slot], 16 * uses_of_slot)

        def ffn_slots(eng, slot):
            for i in range(2 * RING):
                slot(i, i % RING)
            with eng.Fori(2, TILES // RING - 1) as g:
                for r in range(RING):
                    slot(g * RING + r, r)
            for i in range(TILES - RING, TILES):
                slot(i, i % RING)

        HALVES = (slice(0, 2 * H), slice(2 * H, 4 * H))

        def lo_count(load):
            return load if load <= KC else KC + 2 * (load - KC)

        PARTS = 4
        H_STATISTICS, H_NORM, X1_SUM, X1_STATISTICS = range(PARTS)

        def x1_parts_in_slot(i):
            if not isinstance(i, int) or not 1 <= i < PARTS * Q:
                return []
            return [divmod(n, PARTS) for n in ((i - 1,) if i < PARTS * Q - 1 else (i - 1, i))]

        def inside(i, ahead):
            return not isinstance(i, int) or i + ahead < TILES

        @block.sync
        def _(sp):
            def load_x(blk, t, q):
                first_uses = isinstance(t, int) and number(blk, t) == 1 and q < X_SLOTS
                if not is_start(blk, t) and not first_uses:
                    sp.wait_ge(x_turned, Q * number(blk, t) + (q - X_SLOTS + 1))
                sp.dma_start(x_place(blk, t, q), x_rows[bass.ds(row(blk, t, q), P), :]
                             ).then_inc(first_x_loaded[q] if is_start(blk, t) else x_loaded[q % X_SLOTS], 16)

            def load_residual(blk, t, q):
                sp.wait_ge(x1_stored[q % 2], 16 * (Q // 2 * number(blk, t) + q // 2 + CREDIT))
                sp.dma_start(x_res[:, q % 2, :], x_rows[bass.ds(row(blk, t, q), P), :]
                             ).then_inc(x_res_loaded[q % 2], 16)

            def store_x1(blk, t, q):
                sp.wait_ge(x1_stat, 3 * (Q * number(blk, t) + q) + 1)
                sp.dma_start(x1_rows[bass.ds(row(blk, t, q), P), :], x_res[:, q % 2, :]
                             ).then_inc(x1_stored[q % 2], 16)

            def load_weight_rows(rows, load):
                place, count = loads_into(load)
                if place in STAGE_OF_LOAD[:load]:
                    before = max(n for n in range(load) if STAGE_OF_LOAD[n] == place)
                    if before == 0:
                        sp.wait_ge(dft_lo_ready, KC)
                    else:
                        sp.wait_ge(weight_lo_ready, lo_count(before))
                        if before <= KC:
                            sp.wait_ge(weight_lo_by_pool, before)
                sp.dma_start(stages[place], rows).then_inc(stage_loaded[place], 16)

            def load_spectral(r):
                a, b, c, d = raw[r % 2]
                k = P * (r % 2)
                first, second = (wf_real, wf_imag) if r < 2 else (wf_imag, wf_real)
                skip = 1 if k == 0 else 0
                mirror = (wf_real_reversed, wf_imag_reversed)
                for dst, src in ((a, first), (c, second)):
                    if r == 2:
                        sp.dma_start(dst[1:P, :], src[1:P, :]).then_inc(raw_loaded[r], 16)
                    else:
                        sp.dma_start(dst[:], src[k:k + P, :]).then_inc(raw_loaded[r], 16)
                for dst, src in ((b, mirror[first is wf_imag]), (d, mirror[second is wf_imag])):
                    sp.dma_start(dst[skip:P, :], src[k + skip - 1:k + P - 1, :]).then_inc(raw_loaded[r], 16)
                if r == 2:
                    sp.dma_start(a[0:1, :], wf_real[D // 2:D // 2 + 1, :]).then_inc(raw_loaded[r], 16)
                    sp.dma_start(d[0:1, :], wf_imag[D // 2:D // 2 + 1, :]).then_inc(raw_loaded[r], 16)

            def load_basis(r):
                sp.dma_start(stage[0][:, r * D:(r + 1) * D], dft[r * P:(r + 1) * P, :]).then_inc(basis_loaded[r], 16)

            sp.dma_start(bias_rows, gate_bias.rearrange("(c p) -> c p", p=P)).then_inc(bias_loaded, 16)
            for par in range(2):
                sp.sem_inc(x1_stored[par], 16 * CREDIT)
            for r in range(RING):
                sp.sem_inc(out_stored[r], 16 * CREDIT)
            load_spectral(0)
            load_basis(0)
            load_spectral(1)
            load_basis(1)
            sp.wait_ge(cols_folded, 3 * 1)
            load_spectral(2)
            load_basis(2)
            sp.wait_ge(cols_folded, 3 * 2)
            load_spectral(3)
            load_basis(3)
            for q in range(Q):
                load_x(0, 0, q)
            for k in range(KC):
                load_weight_rows(w_rows[k], 1 + k)
            for q in range(X_SLOTS):
                load_x(0, 1, q)
            for k in range(2):
                load_weight_rows(u_rows[k], 1 + KC + k)
            for dc in range(KC):
                sp.wait_ge(m_lo_ready, dc + 1)
                for n, part in enumerate((wf_hi, wf_lo)):
                    sp.dma_start(m_dram[n][:, dc * D:(dc + 1) * D], part[:, dc, :].bitcast(F32)).then_inc(m_spilled, 16)
            load_weight_rows(u_rows[2], 1 + KC + 2)

            def step(blk, t, par):
                start = is_start(blk, t)
                last = is_last(blk, t)
                if not last and not start:
                    load_x(*following(blk, t), 0)
                    load_x(*following(blk, t), 1)
                if not start:
                    load_residual(*preceding(blk, t), 0)
                    load_residual(*preceding(blk, t), 1)
                    store_x1(*preceding(blk, t), 0)
                    load_residual(*preceding(blk, t), 2)
                if not last:
                    load_x(*following(blk, t), 2)
                if start:
                    load_weight_rows(u_rows[3], 1 + KC + 3)
                if not start:
                    store_x1(*preceding(blk, t), 1)
                    load_residual(*preceding(blk, t), 3)
                    store_x1(*preceding(blk, t), 2)
                if not last:
                    load_x(*following(blk, t), 3)
                if not start:
                    store_x1(*preceding(blk, t), 3)

            all_steps(sp, step)

            load_residual(BLOCKS - 1, T - 1, 0)
            load_residual(BLOCKS - 1, T - 1, 1)
            sp.wait_ge(m_spilled, 2 * KC * 16)
            sp.wait_ge(xn_used, STEPS - BLOCKS)

            def load_x1(i, r):
                at_least(sp, out_ready, i - (RING - 1))
                sp.dma_start(x1_tile[:, r, :], x1_rows[bass.ds(i * P, P), :]).then_inc(x1_loaded[r], 16)

            for par in range(2):
                sp.wait_ge(x1_stored[par], 16 * ((TILES - Q) // 2 + CREDIT))
            load_x1(0, 0)
            load_x1(1, 1)
            for k in range(KC):
                for n, part in enumerate((m_hi, m_lo)):
                    sp.dma_start(part[:, k, :].bitcast(F32), m_dram[n][:, k * D:(k + 1) * D]).then_inc(m_loaded[k], 16)
            sp.dma_start(ffn_bias_all[:], ffn_bias.partition_broadcast(P)).then_inc(ffn_bias_loaded, 16)
            for i in range(2, AHEAD):
                load_x1(i, i)

            def store_out(i, r):
                sp.wait_ge(out_ready, i + 1)
                sp.dma_start(out_rows[bass.ds(i * P, P), :], out_tile[:, r, :]).then_inc(out_stored[r], 16)

            def slot(i, r):
                if inside(i, AHEAD):
                    load_x1(i + AHEAD, (r + AHEAD) % RING)
                if not (isinstance(i, int) and i < 2):
                    store_out(i - 2, (r - 2) % RING)
                for q, part in x1_parts_in_slot(i):
                    if part == X1_STATISTICS:
                        store_x1(BLOCKS - 1, T - 1, q)
                        if q + 2 < Q:
                            load_residual(BLOCKS - 1, T - 1, q + 2)
                if isinstance(i, int) and i + AHEAD == TILES - Q - 1:
                    for par in range(2):
                        sp.wait_ge(x1_stored[par], 16 * (TILES // 2 + CREDIT))

            ffn_slots(sp, slot)
            for i in (TILES - 2, TILES - 1):
                store_out(i, i % RING)
            for r in range(RING):
                sp.wait_ge(out_stored[r], 16 * (TILES // RING + CREDIT))

        @block.tensor
        def _(pe):
            def product(bank, lhs_hi, lhs_lo, rhs_hi, rhs_lo, start, stop):
                pe.matmul(bank, lhs_hi, rhs_hi, start=start, stop=False)
                pe.matmul(bank, lhs_hi, rhs_lo, start=False, stop=False)
                return pe.matmul(bank, lhs_lo, rhs_hi, start=False, stop=stop)

            def turn_x(blk, t, q):
                tile = Q * number(blk, t) + q
                pe.wait_ge(x_normed, tile + 1)
                for k in range(KC):
                    mm = pe.transpose(psum[:, TILE_BANK + q, k * P:(k + 1) * P],
                                      x_place(blk, t, q)[:, k * P:(k + 1) * P], ident)
                mm.then_inc(x_turned, 1)

            def turn_h(blk, t, q, bank):
                pe.wait_ge(h_ready, KC * number(blk, t) + KC)
                for k in range(KC):
                    mm = pe.transpose(psum[:, bank, k * P:(k + 1) * P], h_full[:, k, q * P:(q + 1) * P], ident)
                mm.then_inc(h_turned, 1)

            pe.wait_ge(ident_r_ready, 1)
            pe.wait_ge(bias_loaded, 16)
            pe.transpose(psum[:, 0, 0:4 * KC], bias_rows, ident_r[0:4 * KC, 0:4 * KC].bitcast(F32)
                         ).then_inc(bias_turned, 1)
            pe.wait_ge(bias_ready, 1)
            for r in range(KC):
                pe.wait_ge(dft_lo_ready, r + 1)
                pe.wait_ge(wf_lo_ready, r + 1)
                for jj in range(KC):
                    mm = product(psum[:, jj, :], wf_hi[:, r, jj * P:(jj + 1) * P], wf_lo[:, r, jj * P:(jj + 1) * P],
                                 t_hi[:, r, :], t_lo[:, r, :], r == 0, r == KC - 1)
                    if r == KC - 1:
                        mm.then_inc(g_done, 1)
            for dc in range(KC):
                if dc == KC - 1:
                    for q in range(Q):
                        turn_x(0, 0, q)
                for jj in range(KC):
                    if dc == 0:
                        pe.wait_ge(g_lo_ready, jj + 1)
                    mm = product(psum[:, dc, :], g_hi[:, jj, dc * P:(dc + 1) * P], g_lo[:, jj, dc * P:(dc + 1) * P],
                                 t_hi[:, jj, :], t_lo[:, jj, :], jj == 0, jj == KC - 1)
                mm.then_inc(m_done, 1)

            def turn_xn2(i, r):
                pe.wait_ge(xn2_ready, i + 1)
                at_least(pe, xn2_lo_ready, i - 1)
                for k in range(KC):
                    mm = pe.transpose(psum[:, XN2_BANK + r % 2, k * P:(k + 1) * P], xn2[:, r, k * P:(k + 1) * P], ident)
                mm.then_inc(xn2_turned, 1)

            def step(blk, t, par):
                s = number(blk, t)
                first = isinstance(t, int) and t == 0
                last = is_last(blk, t)
                gates = gates_of(t)

                def x_products(j, kind, k, start, stop):
                    col = COLUMN_OF_KIND[kind] * H + j * P
                    return product(psum[:, kind, :], w_hi[:, k, col:col + P], w_lo[:, k, col:col + P],
                                   xn_hi[:, k, :], xn_lo[:, k, :], start, stop)

                def x_part(j, kind):
                    pe.wait_ge(gate_read[kind], uses(kind, blk, t, j) + CREDIT)
                    if is_start(blk, t) and j == 0:
                        pe.wait_ge(m_lo_ready, kind + 1)
                    for k in range(KC):
                        if is_start(blk, t) and j == 0 and kind in (I, C):
                            pe.wait_ge(weight_lo_ready if kind == I else weight_lo_by_pool, k + 1)
                        mm = x_products(j, kind, k, k == 0, first and k == KC - 1)
                    return mm

                def h_products(j, kind, k, start, stop):
                    col = COLUMN_OF_KIND[kind] * H + j * P
                    return product(psum[:, kind, :], u_hi[:, k, col:col + P], u_lo[:, k, col:col + P],
                                   h_hi[1 - par][:, k, :], h_lo[1 - par][:, k, :], start, stop)

                def h_part(j, kind):
                    for k in range(KC):
                        mm = h_products(j, kind, k, False, k == KC - 1)
                    mm.then_inc(gate_done[kind], 1)

                def turn_next_x(q):
                    if not is_start(blk, t):
                        pe.wait_ge(x1_ready, Q * (s - 1) + q + 1)
                    turn_x(*following(blk, t), q)

                def first_gate(kind):
                    pe.wait_ge(gate_read[kind], uses(kind, blk, t, 0) + CREDIT)
                    if blk == 0 and par == 1:
                        pe.wait_ge(weight_lo_ready, lo_count(2 * KC))
                    for k in range(KC - 1):
                        pe.wait_ge(h_lo_ready, KC * (s - 1) + k + 1)
                        h_products(0, kind, k, k == 0, False)
                    pe.wait_ge(xn_lo_ready, Q * s + Q)
                    for k in range(KC):
                        x_products(0, kind, k, False, False)
                    pe.wait_ge(h_lo_ready, KC * s)
                    h_products(0, kind, KC - 1, False, True).then_inc(gate_done[kind], 1)

                turn_h_after = {1: (0, 1), 2: (2, 3)} if first else {0: (0, 1), 1: (2, 3)}
                turn_x_after = {4: 0, 6: 1, 9: 2} if first else {5: 0, 8: 1, 11: 2, 13: 3}
                if first:
                    pe.wait_ge(xn_lo_ready, Q * s + Q)
                for n, (j, kind) in enumerate(gates[:-2]):
                    if first:
                        x_part(j, kind).then_inc(gate_done[kind], 1)
                    elif n == 0:
                        first_gate(kind)
                    else:
                        x_part(j, kind)
                        h_part(j, kind)
                    if n in turn_h_after and not is_start(blk, t):
                        for q in turn_h_after[n]:
                            turn_h(*preceding(blk, t), q, TILE_BANK + q)
                    if n in turn_x_after and not last:
                        turn_next_x(turn_x_after[n])
                pending = gates[-2:]
                for j, kind in pending:
                    mm = x_part(j, kind)
                    if first:
                        mm.then_inc(gate_done[kind], 1)
                if first:
                    turn_next_x(Q - 1)
                else:
                    mm.then_inc(xn_used, 1)
                    for j, kind in pending:
                        h_part(j, kind)

            all_steps(pe, step)

            pe.wait_ge(x1_ready, TILES - Q)
            turn_xn2(0, 0)

            def slot(i, r):
                opening = isinstance(i, int) and i == 0
                if inside(i, 1) and not opening:
                    turn_xn2(i + 1, (r + 1) % RING)
                pe.wait_ge(xn2_lo_ready, i + 1)
                at_least(pe, y_ready, i - 1)
                hi, lo = xn2_hi[r % 2], xn2_lo[r % 2]
                for k in range(KC):
                    if opening:
                        pe.wait_ge(m_loaded[k], 32)
                    mm = product(psum[:, Y_BANK + r % 2, :], hi[:, k, :], lo[:, k, :], m_hi[:, k, :], m_lo[:, k, :],
                                 k == 0, k == KC - 1)
                mm.then_inc(y_done, 1)
                if opening:
                    turn_xn2(1, 1)
                    for q in range(Q):
                        turn_h(BLOCKS - 1, T - 1, q, q)

            ffn_slots(pe, slot)

        @block.scalar
        def _(act):
            for kind in (I, C, F, O):
                act.sem_inc(gate_read[kind], CREDIT)
            act.wait_ge(bias_turned, 1)
            act.copy(bias_cols[:], psum[:, 0, 0:4 * KC]).then_inc(bias_ready, 1)

            def basis_hi(r):
                act.wait_ge(basis_loaded[r], 16)
                act.copy(t_hi[:, r, :], stage[0][:, r * D:(r + 1) * D]).then_inc(dft_hi_ready, 1)

            def folded_hi(r):
                act.wait_ge(cols_folded, 3 * (r + 1))
                act.copy(wf_hi[:, r, :], (gate_a, gate_b)[r % 2][:]).then_inc(wf_hi_ready, 1)

            def weight_hi(dst, k, load):
                place, count = loads_into(load)
                act.wait_ge(stage_loaded[place], 16 * count)
                for half in HALVES:
                    act.copy(dst[:, k, half], stages[place][:, half]).then_inc(weight_hi_ready, 1)

            def input_hi(blk, t, q):
                act.wait_ge(x_turned, Q * number(blk, t) + q + 1)
                act.copy(xn_hi[:, :, q * P:(q + 1) * P], psum[:, TILE_BANK + q, :].rearrange("p (k n) -> p k n", k=KC)
                         ).then_inc(xn_hi_ready, 1)

            basis_hi(0)
            folded_hi(0)
            basis_hi(1)
            folded_hi(1)
            basis_hi(2)
            folded_hi(2)
            basis_hi(3)
            folded_hi(3)
            act.wait_ge(consts_ready, 5)
            for jj in range(KC):
                act.wait_ge(g_done, jj + 1)
                act.activation(g_hi[:, jj, :], psum[:, jj, :], ACT.Copy, scale=dft_scale[:, jj:jj + 1]
                               ).then_inc(g_hi_ready, 1)
            weight_hi(w_hi, 0, 1)
            for dc in range(KC):
                if dc < 2:
                    weight_hi(w_hi, dc + 1, dc + 2)
                if dc == 2:
                    for q in range(Q):
                        input_hi(0, 0, q)
                    weight_hi(w_hi, 3, 4)
                act.wait_ge(m_done, dc + 1)
                act.copy(wf_hi[:, dc, :], psum[:, dc, :]).then_inc(m_hi_ready, 1)

            weight_hi(u_hi, 0, 1 + KC)
            weight_hi(u_hi, 1, 2 + KC)

            def norm_x1(i, r):
                act.wait_ge(x1_loaded[r], 16 // RING * (i - r) + 16)
                at_least(act, xn2_turned, i - (RING - 1))
                if isinstance(i, int) and i == 0:
                    act.wait_ge(x1_centre_ready, TILES - Q + CREDIT)
                if isinstance(i, int) and i == TILES - Q:
                    act.wait_ge(x1_centre_ready, TILES + CREDIT)
                act.activation(xn2[:, r, :], x1_tile[:, r, :], ACT.Identity,
                               bias=x1_centre[:, bass.ds(i, 1), :].rearrange("p a b -> p (a b)"),
                               scale=x1_rstd[:, bass.ds(i, 1), :].rearrange("p a b -> p (a b)")
                               ).then_inc(xn2_ready, 1)

            def step(blk, t, par):
                s = number(blk, t)
                first = isinstance(t, int) and t == 0
                last = is_last(blk, t)

                def gate(j, kind, dst):
                    act.wait_ge(gate_done[kind], uses(kind, blk, t, j) + 1)
                    col = COLUMN_OF_KIND[kind] * KC + j
                    act.activation(dst[:], psum[:, kind, :], ACT.Tanh if kind == C else ACT.Sigmoid,
                                   bias=bias_cols[:, col:col + 1]).then_inc(gate_read[kind], 1)

                for j in range(KC):
                    n = KC * s + j
                    gate(j, I, gate_a)
                    if last:
                        act.wait_ge(h_ready, n)
                    gate(j, C, gate_b)
                    if j == KC - 1 and not last:
                        if first:
                            act.wait_ge(gate_done[O], uses(O, blk, t, j) + 1)
                        else:
                            act.wait_ge(xn_used, s - blk)
                        for q in range(Q):
                            input_hi(*following(blk, t), q)
                    if not first:
                        gate(j, F, gate_c)
                    if last and j == KC - 1:
                        norm_x1(0, 0)
                    act.wait_ge(c_ready, n + 1)
                    act.activation(gate_b[:], c_state[:, j, :], ACT.Tanh).then_inc(tanh_c_ready, 1)
                    gate(j, O, gate_c)
                    if not last:
                        act.wait_ge(h_ready, n + 1)
                        act.copy(h_hi[par][:, j, :], h_full[:, j, :]).then_inc(h_hi_ready, 1)
                    if is_start(blk, t) and j < 2:
                        if j == 0:
                            act.wait_ge(m_spilled, 2 * KC * 16)
                        weight_hi(u_hi, 2 + j, 1 + KC + 2 + j)

            all_steps(act, step)

            def y_norm(i, r):
                act.wait_ge(y_centre_ready, i + 1)
                act.activation(y_tile[:, r, :], y_tile[:, r, :], ACT.Identity, bias=y_centre[:, r % 2, :],
                               scale=y_rstd[:, r % 2, :]).then_inc(y_normed, 1)

            def slot(i, r):
                if inside(i, 1):
                    xn2_part(i + 1, r + 1)
                if inside(i, 3):
                    norm_x1(i + 3, (r + 3) % RING)
                if not (isinstance(i, int) and i == 0):
                    y_norm(i - 1, (r - 1) % RING)

            def xn2_part(i, r):
                act.wait_ge(xn2_turned, i + 1)
                at_least(act, y_done, i - 1)
                act.copy(xn2_hi[r % 2][:].rearrange("p k n -> p (k n)"), psum[:, XN2_BANK + r % 2, :]
                         ).then_inc(xn2_hi_ready, 1)

            xn2_part(0, 0)
            norm_x1(1, 1)
            norm_x1(2, 2)
            ffn_slots(act, slot)
            y_norm(TILES - 1, (TILES - 1) % RING)

        @block.vector
        def _(dve):
            dve.wait_ge(ident_made, 1)
            dve.tensor_copy(ident_r[:], ident_made_in).then_inc(ident_r_ready, 1)
            dve.wait_ge(consts_ready, 5)

            def norm_x(blk, t, q):
                x_statistics(blk, t, q)
                x_from_statistics(blk, t, q)

            def x_statistics(blk, t, q):
                tile = Q * number(blk, t) + q
                x_is_loaded(dve, blk, t, q)
                dve.bn_stats(x_bn[:], x_place(blk, t, q)).then_inc(x_stat, 1)
                dve.wait_ge(x_stat, 3 * tile + 1)
                dve.sem_inc(stats_seen, 1)
                dve.bn_aggr(x_mv[:, q, :], x_bn[:]).then_inc(x_stat, 1)
                dve.wait_ge(x_stat, 3 * tile + 2)
                dve.tensor_scalar_add(x_ve[:, q, :], x_mv[:, q, 1:2], EPS).then_inc(x_stat, 1)

            def x_from_statistics(blk, t, q):
                tile = Q * number(blk, t) + q
                dve.wait_ge(x_rstd_ready, tile + 1)
                dve.tensor_scalar(x_place(blk, t, q), x_place(blk, t, q), x_mv[:, q, 0:1], x_rstd[:, q, :],
                                  ALU.subtract, ALU.mult).then_inc(x_normed, 1)

            def input_lo(blk, t, q):
                dve.wait_ge(xn_hi_ready, Q * number(blk, t) + q + 1)
                part = (slice(None), slice(None), slice(q * P, (q + 1) * P))
                dve.tensor_sub(xn_lo[part], psum[:, TILE_BANK + q, :].rearrange("p (k n) -> p k n", k=KC),
                               xn_hi[part].bitcast(F32)).then_inc(xn_lo_ready, 1)

            def fold(r):
                a, b, c, d = raw[r % 2]
                op = ALU.add if r < 2 else ALU.subtract
                dve.wait_ge(raw_loaded[r], 16 * (6 if r == 2 else 4))
                dve.wait_ge(edge_zeroed, 3 if r == 2 else 2)
                dve.tensor_tensor(a[:], a[:], b[:], op).then_inc(rows_folded, 1)
                dve.tensor_tensor(c[:], d[:], c[:], op).then_inc(rows_folded, 1)
                dve.wait_ge(rows_folded, 2 * r + 2)
                at_least(dve, wf_lo_ready, r - 1)
                f = (gate_a, gate_b)[r % 2]
                half = D // 2
                dve.tensor_copy(f[:, 0:D:half], a[:, 0:D:half]).then_inc(cols_folded, 1)
                dve.tensor_tensor(f[:, 1:half], a[:, 1:half], a[:, D - 1:half:-1], ALU.add).then_inc(cols_folded, 1)
                dve.tensor_tensor(f[:, half + 1:D], c[:, 1:half], c[:, D - 1:half:-1], ALU.subtract
                                  ).then_inc(cols_folded, 1)

            def folded_lo(r):
                dve.wait_ge(wf_hi_ready, r + 1)
                dve.tensor_sub(wf_lo[:, r, :], (gate_a, gate_b)[r % 2][:], wf_hi[:, r, :].bitcast(F32)
                               ).then_inc(wf_lo_ready, 1)

            def weight_lo(dst_hi, dst, k, load):
                place, count = loads_into(load)
                for n, half in enumerate(HALVES[:1] if load <= KC else HALVES):
                    dve.wait_ge(weight_hi_ready, 2 * (load - 1) + n + 1)
                    dve.tensor_sub(dst[:, k, half], stages[place][:, half], dst_hi[:, k, half].bitcast(F32)
                                   ).then_inc(weight_lo_ready, 1)

            fold(0)
            folded_lo(0)
            fold(1)
            folded_lo(1)
            fold(2)
            folded_lo(2)
            fold(3)
            folded_lo(3)
            x_statistics(0, 0, 0)
            x_statistics(0, 0, 1)
            for jj in range(KC):
                dve.wait_ge(g_hi_ready, jj + 1)
                dve.scalar_tensor_tensor(out=g_lo[:, jj, :], in0=psum[:, jj, :], scalar=dft_scale[:, jj:jj + 1],
                                         in1=g_hi[:, jj, :].bitcast(F32), op0=ALU.mult, op1=ALU.subtract
                                         ).then_inc(g_lo_ready, 1)
            x_statistics(0, 0, 2)
            x_statistics(0, 0, 3)
            for q in range(Q):
                x_from_statistics(0, 0, q)
            weight_lo(w_hi, w_lo, 0, 1)
            weight_lo(w_hi, w_lo, 1, 2)
            for dc in range(KC):
                if dc == 2:
                    weight_lo(w_hi, w_lo, 2, 3)
                    for q in range(Q):
                        input_lo(0, 0, q)
                    weight_lo(w_hi, w_lo, 3, 4)
                dve.wait_ge(m_hi_ready, dc + 1)
                dve.tensor_sub(wf_lo[:, dc, :], psum[:, dc, :], wf_hi[:, dc, :].bitcast(F32)).then_inc(m_lo_ready, 1)

            weight_lo(u_hi, u_lo, 0, 1 + KC)

            def h_statistics(blk, t, q, bank):
                tile = Q * number(blk, t) + q
                dve.wait_ge(h_turned, tile + 1)
                dve.bn_stats(h_bn[:], psum[:, bank, :]).then_inc(h_stat, 1)
                dve.wait_ge(h_stat, 3 * tile + 1)
                dve.sem_inc(stats_seen, 1)
                dve.bn_aggr(h_mv[:], h_bn[:]).then_inc(h_stat, 1)
                dve.wait_ge(h_stat, 3 * tile + 2)
                dve.tensor_scalar_add(h_ve[:], h_mv[:, 1:2], EPS).then_inc(h_stat, 1)

            def residual(blk, t, q, bank):
                h_statistics(blk, t, q, bank)
                x1_and_statistics(blk, t, q, bank)

            def x1_and_statistics(blk, t, q, bank):
                h_norm(blk, t, q, bank)
                x1_sum(blk, t, q, bank)
                x1_statistics(blk, t, q)

            def h_norm(blk, t, q, bank):
                tile = Q * number(blk, t) + q
                dve.wait_ge(h_rstd_ready, tile + 1)
                dve.tensor_scalar(psum[:, bank, :], psum[:, bank, :], h_mv[:, 0:1], h_rstd[:],
                                  ALU.subtract, ALU.mult).then_inc(h_normed, 1)

            def x1_sum(blk, t, q, bank):
                tile = Q * number(blk, t) + q
                b = q % 2
                dve.wait_ge(h_normed, tile + 1)
                dve.wait_ge(x_res_loaded[b], 16 * (Q // 2 * number(blk, t) + q // 2 + 1))
                dve.tensor_tensor(x_res[:, b, :], psum[:, bank, :], x_res[:, b, :], ALU.add).then_inc(x1_ready, 1)

            def x1_statistics(blk, t, q):
                tile = Q * number(blk, t) + q
                b = q % 2
                dve.wait_ge(x1_ready, tile + 1)
                dve.bn_stats(x1_bn[:], x_res[:, b, :]).then_inc(x1_stat, 1)
                dve.wait_ge(x1_stat, 3 * tile + 1)
                dve.wait_ge(x1_centre_ready, tile + CREDIT)
                dve.sem_inc(stats_seen, 1)
                dve.bn_aggr(x1_mv[:], x1_bn[:]).then_inc(x1_stat, 1)
                dve.wait_ge(x1_stat, 3 * tile + 2)
                dve.tensor_scalar_add(x1_ve[:], x1_mv[:, 1:2], EPS).then_inc(x1_stat, 1)

            def step(blk, t, par):
                s = number(blk, t)
                first = isinstance(t, int) and t == 0
                start = is_start(blk, t)
                last = is_last(blk, t)
                for j in range(KC):
                    n = KC * s + j
                    if not last and j == 0:
                        norm_x(*following(blk, t), 0)
                    dve.wait_ge(gate_read[I], n + 1 + CREDIT)
                    dve.wait_ge(gate_read[C], n + 1 + CREDIT)
                    if first:
                        dve.tensor_mul(c_state[:, j, :], gate_a[:], gate_b[:]).then_inc(c_ready, 1)
                    else:
                        dve.tensor_mul(gate_a[:], gate_a[:], gate_b[:]).then_inc(ic_ready, 1)
                    turned, tile = not start and j < 3, (0, 1, 3, None)[j]
                    if turned:
                        h_statistics(*preceding(blk, t), tile, TILE_BANK + tile)
                    if not last and j < 3:
                        x_statistics(*following(blk, t), j + 1)
                    if turned:
                        x1_and_statistics(*preceding(blk, t), tile, TILE_BANK + tile)
                    if not last and j < 3:
                        x_from_statistics(*following(blk, t), j + 1)
                    if j == KC - 1 and not last:
                        for q in range(Q):
                            input_lo(*following(blk, t), q)
                    if not first:
                        done = uses(F, blk, t, j) + 1
                        dve.wait_ge(gate_read[F], done + CREDIT)
                        dve.tensor_mul(gate_c[:], gate_c[:], c_state[:, j, :]).then_inc(fc_ready, 1)
                        dve.wait_ge(fc_ready, done)
                        dve.wait_ge(ic_ready, done)
                        dve.tensor_add(c_state[:, j, :], gate_c[:], gate_a[:]).then_inc(c_ready, 1)
                    dve.wait_ge(tanh_c_ready, n + 1)
                    dve.wait_ge(gate_read[O], n + 1 + CREDIT)
                    if j == 0:
                        if start:
                            dve.wait_ge(x_turned, Q)
                        else:
                            dve.wait_ge(h_turned, Q * s)
                    dve.tensor_mul(h_full[:, j, :], gate_b[:], gate_c[:]).then_inc(h_ready, 1)
                    if not last:
                        dve.wait_ge(h_hi_ready, n + 1)
                        dve.tensor_sub(h_lo[par][:, j, :], h_full[:, j, :], h_hi[par][:, j, :].bitcast(F32)
                                       ).then_inc(h_lo_ready, 1)
                    if not start and j == 1:
                        residual(*preceding(blk, t), 2, TILE_BANK + 2)
                    if start and j < KC - 1:
                        weight_lo(u_hi, u_lo, j + 1, 2 + KC + j)

            all_steps(dve, step)

            def lo_xn2(i, r):
                dve.wait_ge(xn2_hi_ready, i + 1)
                dve.tensor_sub(xn2_lo[r % 2][:].rearrange("p k n -> p (k n)"), psum[:, XN2_BANK + r % 2, :],
                               xn2_hi[r % 2][:].rearrange("p k n -> p (k n)").bitcast(F32)).then_inc(xn2_lo_ready, 1)

            lo_xn2(0, 0)
            dve.wait_ge(ffn_bias_loaded, 16)

            def slot(i, r):
                if inside(i, 1):
                    lo_xn2(i + 1, (r + 1) % RING)
                for q, part in x1_parts_in_slot(i):
                    if part == H_STATISTICS:
                        h_statistics(BLOCKS - 1, T - 1, q, q)
                    elif part == H_NORM:
                        h_norm(BLOCKS - 1, T - 1, q, q)
                    elif part == X1_SUM:
                        x1_sum(BLOCKS - 1, T - 1, q, q)
                    else:
                        x1_statistics(BLOCKS - 1, T - 1, q)
                b = r % 2
                dve.wait_ge(y_done, i + 1)
                at_least(dve, out_ready, i - (RING - 1))
                dve.tensor_add(y_tile[:, r, :], psum[:, Y_BANK + b, :], ffn_bias_all[:]).then_inc(y_ready, 1)
                dve.wait_ge(y_ready, i + 1)
                dve.bn_stats(y_bn[:], y_tile[:, r, :]).then_inc(y_stat, 1)
                at_least(dve, y_centre_ready, i - 1)
                dve.wait_ge(y_stat, 3 * i + 1)
                dve.sem_inc(stats_seen, 1)
                dve.bn_aggr(y_mv[:, b, :], y_bn[:]).then_inc(y_stat, 1)
                dve.wait_ge(y_stat, 3 * i + 2)
                dve.tensor_scalar_add(y_ve[:, b, :], y_mv[:, b, 1:2], EPS).then_inc(y_stat, 1)

            ffn_slots(dve, slot)

        @block.gpsimd
        def _(pool):
            pool.sem_inc(x1_centre_ready, CREDIT)
            pool.memset(ident_made_in, 0.0).then_inc(ident_zeroed, 1)
            pool.wait_ge(ident_zeroed, 1)
            pool.affine_select(out=ident_made_in, in_=ident_made_in, compare_op=ALU.not_equal, fill=1.0, base=0,
                               pattern=[[-1, P]], channel_multiplier=1).then_inc(ident_made, 1)
            pool.memset(minus_half[:], -0.5).then_inc(consts_ready, 1)
            pool.wait_ge(consts_ready, 1)
            pool.memset(zero[:], 0.0).then_inc(consts_ready, 1)
            pool.memset(dft_scale[:, 0:KC // 2], 1.0 / D).then_inc(consts_ready, 1)
            pool.memset(dft_scale[:, KC // 2:KC], -1.0 / D).then_inc(consts_ready, 1)
            pool.wait_ge(consts_ready, 4)
            pool.memset(dft_scale[0:1, KC // 2:KC // 2 + 1], 1.0 / D).then_inc(consts_ready, 1)
            pool.memset(raw[0][1][0:1, :], 0.0).then_inc(edge_zeroed, 1)
            pool.memset(raw[0][3][0:1, :], 0.0).then_inc(edge_zeroed, 1)

            def rstd_x(blk, t, q):
                tile = Q * number(blk, t) + q
                pool.wait_ge(x_stat, 3 * tile + 3)
                pool.tensor_tensor(x_rstd[:, q, :], x_ve[:, q, :], minus_half[:], ALU.pow
                                   ).then_inc(x_rstd_ready, 1)

            def rstd_h(blk, t, q):
                tile = Q * number(blk, t) + q
                pool.wait_ge(h_stat, 3 * tile + 3)
                pool.tensor_tensor(h_rstd[:], h_ve[:], minus_half[:], ALU.pow).then_inc(h_rstd_ready, 1)

            def rstd_x1(blk, t, q):
                tile = Q * number(blk, t) + q
                pool.wait_ge(x1_stat, 3 * tile + 3)
                at = t * (B // P) + (blk * Q + q)
                pool.tensor_tensor(x1_rstd[:, bass.ds(at, 1), :].rearrange("p a b -> p (a b)"),
                                   x1_ve[:], minus_half[:], ALU.pow).then_inc(x1_rstd_ready, 1)
                pool.wait_ge(x1_rstd_ready, tile + 1)
                pool.sem_inc(rstd_seen, 1)
                pool.tensor_tensor(x1_scaled_mean[:], x1_mv[:, 0:1],
                                   x1_rstd[:, bass.ds(at, 1), :].rearrange("p a b -> p (a b)"), ALU.mult
                                   ).then_inc(x1_scaled_mean_ready, 1)
                pool.wait_ge(x1_scaled_mean_ready, tile + 1)
                pool.sem_inc(rstd_seen, 1)
                pool.tensor_tensor(x1_centre[:, bass.ds(at, 1), :].rearrange("p a b -> p (a b)"),
                                   zero[:], x1_scaled_mean[:], ALU.subtract).then_inc(x1_centre_ready, 1)

            def rstd_residual(blk, t, q):
                rstd_h(blk, t, q)
                rstd_x1(blk, t, q)

            def basis_lo(r):
                pool.wait_ge(dft_hi_ready, r + 1)
                pool.tensor_tensor(t_lo[:, r, :], stage[0][:, r * D:(r + 1) * D], t_hi[:, r, :].bitcast(F32),
                                   ALU.subtract).then_inc(dft_lo_ready, 1)

            basis_lo(0)
            pool.wait_ge(cols_folded, 3)
            pool.memset(raw[0][2][0:1, :], 0.0).then_inc(edge_zeroed, 1)
            for r in range(1, KC):
                basis_lo(r)
            for q in range(Q):
                rstd_x(0, 0, q)
            for k in range(KC):
                place, count = loads_into(1 + k)
                pool.wait_ge(weight_hi_ready, 2 * (k + 1))
                pool.tensor_tensor(w_lo[:, k, HALVES[1]], stages[place][:, HALVES[1]],
                                   w_hi[:, k, HALVES[1]].bitcast(F32), ALU.subtract).then_inc(weight_lo_by_pool, 1)

            def step(blk, t, par):
                start = isinstance(t, int) and t == 0 and blk == 0
                last = is_last(blk, t)
                for j in range(KC):
                    if not last and j == 0:
                        rstd_x(*following(blk, t), 0)
                    turned, tile = not start and j < 3, (0, 1, 3, None)[j]
                    if turned:
                        rstd_h(*preceding(blk, t), tile)
                    if not last and j < 3:
                        rstd_x(*following(blk, t), j + 1)
                    if turned:
                        rstd_x1(*preceding(blk, t), tile)
                    if not start and j == 1:
                        rstd_residual(*preceding(blk, t), 2)

            all_steps(pool, step)

            def add_up(i, r):
                pool.wait_ge(y_normed, i + 1)
                pool.wait_ge(out_stored[r], 16 // RING * (i - r) + 16 * CREDIT)
                pool.tensor_tensor(out_tile[:, r, :], y_tile[:, r, :], x1_tile[:, r, :], ALU.add
                                   ).then_inc(out_ready, 1)

            def slot(i, r):
                for q, part in x1_parts_in_slot(i):
                    if part == H_STATISTICS:
                        rstd_h(BLOCKS - 1, T - 1, q)
                    if part == X1_STATISTICS:
                        rstd_x1(BLOCKS - 1, T - 1, q)
                pool.wait_ge(y_stat, 3 * i + 3)
                at_least(pool, y_normed, i - 1)
                pool.tensor_tensor(y_rstd[:, r % 2, :], y_ve[:, r % 2, :], minus_half[:], ALU.pow
                                   ).then_inc(y_rstd_ready, 1)
                pool.wait_ge(y_rstd_ready, i + 1)
                pool.tensor_tensor(y_scaled_mean[:], y_mv[:, r % 2, 0:1], y_rstd[:, r % 2, :], ALU.mult
                                   ).then_inc(y_scaled_mean_ready, 1)
                pool.wait_ge(y_scaled_mean_ready, i + 1)
                pool.tensor_tensor(y_centre[:, r % 2, :], zero[:], y_scaled_mean[:], ALU.subtract
                                   ).then_inc(y_centre_ready, 1)
                if not (isinstance(i, int) and i == 0):
                    add_up(i - 1, (r - 1) % RING)

            ffn_slots(pool, slot)
            add_up(TILES - 1, (TILES - 1) % RING)


_INS = ["L0_attn_input_seq", "L0_attn_w", "L0_attn_u", "L0_attn_bias",
        "L0_ffn_w_freq_real", "L0_ffn_w_freq_imag", "L0_ffn_bias"]


def _real_fourier_basis(n):
    import numpy as np

    kd = np.outer(np.arange(n // 2 + 1), np.arange(n)) % n
    angle = 2.0 * np.pi * kd / n
    return np.concatenate([np.cos(angle), np.sin(angle[1:n // 2])]).astype(np.float32)


def kernel(**inputs):
    import numpy as _np
    import concourse.bacc as _bacc
    from concourse import mybir as _mybir
    from concourse.bass_utils import run_bass_kernel_spmd as _run

    nc = _bacc.Bacc("TRN2", target_bir_lowering=False, num_devices=1)
    arrays, args = {}, []
    for name in _INS:
        a = _np.ascontiguousarray(inputs[name])
        arrays[f"in_{name}_dram"] = a
        args.append(nc.dram_tensor(f"in_{name}_dram", a.shape, _mybir.dt.from_np(a.dtype), kind="ExternalInput").ap())
    for name in ("L0_ffn_w_freq_real", "L0_ffn_w_freq_imag"):
        a = _np.ascontiguousarray(inputs[name][::-1])
        arrays[f"in_{name}_reversed_dram"] = a
        args.append(nc.dram_tensor(f"in_{name}_reversed_dram", a.shape, _mybir.dt.from_np(a.dtype),
                                   kind="ExternalInput").ap())
    basis = _real_fourier_basis(inputs["L0_ffn_w_freq_real"].shape[0])
    arrays["fourier_basis_dram"] = basis
    args.append(nc.dram_tensor("fourier_basis_dram", basis.shape, _mybir.dt.float32, kind="ExternalInput").ap())
    shape = tuple(inputs["L0_attn_input_seq"].shape)
    args.append(nc.dram_tensor("out_0_dram", shape, _mybir.dt.float32, kind="ExternalOutput").ap())
    build(nc, *args)
    r = _run(nc, [arrays], core_ids=[0])
    return r.results[0]["out_0_dram"]
```
